# Optimizing a Trainium2 kernel written in Bass

```python
import numpy as np
import jax
import jax.numpy as jnp

def _softmax(x, axis=-1):
    return jax.nn.softmax(x, axis=axis)

def _gelu(x):
    return jax.nn.gelu(x, approximate=True)

def _silu(x):
    return jax.nn.silu(x)

def _sigmoid(x):
    return jax.nn.sigmoid(x)

def _layernorm(x, axis=-1, eps=1e-05):
    m = jnp.mean(x, axis=axis, keepdims=True)
    v = jnp.var(x, axis=axis, keepdims=True)
    return (x - m) / jnp.sqrt(v + eps)

def _scatter_add(tgt, idx, src, axis=0):
    return tgt.at[idx].add(src)

def _segment_sum(src, seg, n):
    return jax.ops.segment_sum(src, seg, n)
kernel_name = 'mk_adj_seq_d2_adj_r2_f191fb'

def setup_inputs(seed: int=0):
    np.random.seed(seed)
    _w = jnp.asarray

    def _rec_inputs():
        import jax
        import jax.numpy as jnp
        _gk = jax.random.key(seed)
        x = -0.0005207 + 1.001 * jax.random.normal(jax.random.fold_in(_gk, 1), (64, 128, 256), jnp.float32)
        _a = jax.random.bernoulli(jax.random.fold_in(_gk, 2), 0.0625, (64, 128, 128))
        _a = jnp.logical_or(_a, jnp.eye(128, dtype=bool))
        adj = _a.astype(jnp.int32)
        return (x, adj)
    x, adj = _rec_inputs()

    def _L0_gnn_setup():
        import jax, jax.numpy as jnp
        import numpy as np
        B, S, D, H = (2, 1024, 256, 8)
        HD = D // H
        EPS = 1e-05

        def _ln(x, g, b):
            mu = jnp.mean(x, axis=-1, keepdims=True)
            var = jnp.mean((x - mu) ** 2, axis=-1, keepdims=True)
            return (x - mu) * jax.lax.rsqrt(var + EPS) * g + b
        key = jax.random.key(seed)
        ks = jax.random.split(key, 16)
        x = jax.random.normal(ks[0], (B, S, D), dtype=jnp.float32)
        adj = jax.random.randint(ks[1], (B, S, S), 0, 2, dtype=jnp.int32)
        adj = adj.at[:, jnp.arange(S), jnp.arange(S)].set(1)
        edge_attr = jax.random.normal(ks[2], (B, S, S), dtype=jnp.float32)
        sc = 1.0 / np.sqrt(D)
        p = lambda k, shp: jax.random.normal(k, shp, dtype=jnp.float32) * sc
        return {'x': x, 'adj_matrix': adj, 'edge_attr_matrix': edge_attr, 'ln1_g': jnp.ones((D,)), 'ln1_b': jnp.zeros((D,)), 'ln2_g': jnp.ones((D,)), 'ln2_b': jnp.zeros((D,)), 'wq': p(ks[3], (D, D)), 'bq': jnp.zeros((D,)), 'wk': p(ks[4], (D, D)), 'bk': jnp.zeros((D,)), 'wv': p(ks[5], (D, D)), 'bv': jnp.zeros((D,)), 'wo': p(ks[6], (D, D)), 'bo': jnp.zeros((D,)), 'w1': p(ks[7], (D, 4 * D)), 'b1': jnp.zeros((4 * D,)), 'w2': p(ks[8], (4 * D, D)), 'b2': jnp.zeros((D,))}
    _L0_gnn_all = _L0_gnn_setup()
    _L0_gnn_in = {k: v for k, v in _L0_gnn_all.items() if k in ('ln1_g', 'ln1_b', 'ln2_g', 'ln2_b', 'wq', 'bq', 'wk', 'bk', 'wv', 'bv', 'wo', 'bo', 'w1', 'b1', 'w2', 'b2')}
    del _L0_gnn_all

    def _L1_gnn_setup():
        import jax, jax.numpy as jnp
        import numpy as np
        import math
        D = 256
        B, L = (8, 1024)
        EPS = 1e-05

        def layer_norm(y, gamma, beta):
            mu = jnp.mean(y, axis=-1, keepdims=True)
            var = jnp.mean(jnp.square(y - mu), axis=-1, keepdims=True)
            return (y - mu) * jax.lax.rsqrt(var + EPS) * gamma + beta
        key = jax.random.key(seed)
        ks = jax.random.split(key, 8)
        s = 1.0 / math.sqrt(D)
        x = jax.random.normal(ks[0], (B, L, D), dtype=jnp.float32)
        adj = jax.random.randint(ks[1], (B, L, L), 0, 2, dtype=jnp.int32)
        Wq = jax.random.normal(ks[2], (D, D), dtype=jnp.float32) * s
        Wk = jax.random.normal(ks[3], (D, D), dtype=jnp.float32) * s
        Wv = jax.random.normal(ks[4], (D, D), dtype=jnp.float32) * s
        Wo = jax.random.normal(ks[5], (D, D), dtype=jnp.float32) * s
        bo = jnp.zeros((D,), dtype=jnp.float32)
        gamma = jnp.ones((D,), dtype=jnp.float32)
        beta = jnp.zeros((D,), dtype=jnp.float32)
        return {'x': x, 'adj': adj, 'Wq': Wq, 'Wk': Wk, 'Wv': Wv, 'Wo': Wo, 'bo': bo, 'gamma': gamma, 'beta': beta}
    _L1_gnn_all = _L1_gnn_setup()
    _L1_gnn_in = {k: v for k, v in _L1_gnn_all.items() if k in ('Wq', 'Wk', 'Wv', 'Wo', 'bo', 'gamma', 'beta')}
    del _L1_gnn_all
    return {'x': x, 'adj': adj, 'L0_gnn_ln1_g': _L0_gnn_in['ln1_g'], 'L0_gnn_ln1_b': _L0_gnn_in['ln1_b'], 'L0_gnn_ln2_g': _L0_gnn_in['ln2_g'], 'L0_gnn_ln2_b': _L0_gnn_in['ln2_b'], 'L0_gnn_wq': _L0_gnn_in['wq'], 'L0_gnn_bq': _L0_gnn_in['bq'], 'L0_gnn_wk': _L0_gnn_in['wk'], 'L0_gnn_bk': _L0_gnn_in['bk'], 'L0_gnn_wv': _L0_gnn_in['wv'], 'L0_gnn_bv': _L0_gnn_in['bv'], 'L0_gnn_wo': _L0_gnn_in['wo'], 'L0_gnn_bo': _L0_gnn_in['bo'], 'L0_gnn_w1': _L0_gnn_in['w1'], 'L0_gnn_b1': _L0_gnn_in['b1'], 'L0_gnn_w2': _L0_gnn_in['w2'], 'L0_gnn_b2': _L0_gnn_in['b2'], 'L1_gnn_Wq': _L1_gnn_in['Wq'], 'L1_gnn_Wk': _L1_gnn_in['Wk'], 'L1_gnn_Wv': _L1_gnn_in['Wv'], 'L1_gnn_Wo': _L1_gnn_in['Wo'], 'L1_gnn_bo': _L1_gnn_in['bo'], 'L1_gnn_gamma': _L1_gnn_in['gamma'], 'L1_gnn_beta': _L1_gnn_in['beta']}

def reference(x, adj, L0_gnn_ln1_g, L0_gnn_ln1_b, L0_gnn_ln2_g, L0_gnn_ln2_b, L0_gnn_wq, L0_gnn_bq, L0_gnn_wk, L0_gnn_bk, L0_gnn_wv, L0_gnn_bv, L0_gnn_wo, L0_gnn_bo, L0_gnn_w1, L0_gnn_b1, L0_gnn_w2, L0_gnn_b2, L1_gnn_Wq, L1_gnn_Wk, L1_gnn_Wv, L1_gnn_Wo, L1_gnn_bo, L1_gnn_gamma, L1_gnn_beta):
    import jax
    import jax.numpy as jnp

    def _L0_gnn_ref(x, adj_matrix, edge_attr_matrix, ln1_g, ln1_b, ln2_g, ln2_b, wq, bq, wk, bk, wv, bv, wo, bo, w1, b1, w2, b2):
        import jax, jax.numpy as jnp
        import numpy as np
        B, S, D, H = (2, 1024, 256, 8)
        HD = D // H
        EPS = 1e-05

        def _ln(x, g, b):
            mu = jnp.mean(x, axis=-1, keepdims=True)
            var = jnp.mean((x - mu) ** 2, axis=-1, keepdims=True)
            return (x - mu) * jax.lax.rsqrt(var + EPS) * g + b
        b, s, d = x.shape
        residual = x
        nx = _ln(x, ln1_g, ln1_b)
        q = (nx @ wq + bq).reshape(b, s, H, HD).transpose(0, 2, 1, 3)
        k = (nx @ wk + bk).reshape(b, s, H, HD).transpose(0, 2, 1, 3)
        v = (nx @ wv + bv).reshape(b, s, H, HD).transpose(0, 2, 1, 3)
        adjf = adj_matrix.astype(jnp.float32)
        bias = jnp.where(adj_matrix > 0, 0.1 * edge_attr_matrix * adjf, -jnp.inf)[:, None]
        scores = jnp.einsum('bhqd,bhkd->bhqk', q, k) / np.sqrt(HD) + bias
        attn = jax.nn.softmax(scores, axis=-1)
        out = jnp.einsum('bhqk,bhkd->bhqd', attn, v)
        out = out.transpose(0, 2, 1, 3).reshape(b, s, d)
        x1 = residual + (out @ wo + bo)
        n2 = _ln(x1, ln2_g, ln2_b)
        mlp = jax.nn.gelu(n2 @ w1 + b1, approximate=False) @ w2 + b2
        return x1 + mlp

    def _L1_gnn_ref(x, adj, Wq, Wk, Wv, Wo, bo, gamma, beta):
        import jax, jax.numpy as jnp
        import numpy as np
        import math
        D = 256
        B, L = (8, 1024)
        EPS = 1e-05

        def layer_norm(y, gamma, beta):
            mu = jnp.mean(y, axis=-1, keepdims=True)
            var = jnp.mean(jnp.square(y - mu), axis=-1, keepdims=True)
            return (y - mu) * jax.lax.rsqrt(var + EPS) * gamma + beta
        d_out = Wq.shape[1]
        scale = 1.0 / math.sqrt(d_out)
        Q = x @ Wq
        K = x @ Wk
        V = x @ Wv
        sc = jnp.einsum('bld,bmd->blm', Q, K) * scale
        mask = adj == 0
        sc = jnp.where(mask, -jnp.inf, sc)
        all_inf = jnp.all(mask, axis=-1, keepdims=True)
        sc = jnp.where(all_inf, 0.0, sc)
        w = jax.nn.softmax(sc, axis=-1)
        out = jnp.einsum('blm,bmd->bld', w, V)
        y = x + out @ Wo + bo
        return layer_norm(y, gamma, beta)
    x = _L0_gnn_ref(x, adj, adj, L0_gnn_ln1_g, L0_gnn_ln1_b, L0_gnn_ln2_g, L0_gnn_ln2_b, L0_gnn_wq, L0_gnn_bq, L0_gnn_wk, L0_gnn_bk, L0_gnn_wv, L0_gnn_bv, L0_gnn_wo, L0_gnn_bo, L0_gnn_w1, L0_gnn_b1, L0_gnn_w2, L0_gnn_b2)
    x = _L1_gnn_ref(x, adj, L1_gnn_Wq, L1_gnn_Wk, L1_gnn_Wv, L1_gnn_Wo, L1_gnn_bo, L1_gnn_gamma, L1_gnn_beta)
    return x

_drawn_inputs = setup_inputs


def setup_inputs(seed=0):
    import zlib

    import numpy as np

    out = dict(_drawn_inputs(seed))
    spreads = {'L0_gnn_ln1_g': (1.0, 0.2),
     'L0_gnn_ln1_b': (0.0, 0.1),
     'L0_gnn_ln2_g': (1.0, 0.2),
     'L0_gnn_ln2_b': (0.0, 0.1),
     'L0_gnn_bq': (0.0, 0.1),
     'L0_gnn_bk': (0.0, 0.1),
     'L0_gnn_bv': (0.0, 0.1),
     'L0_gnn_bo': (0.0, 0.1),
     'L0_gnn_b1': (0.0, 0.1),
     'L0_gnn_b2': (0.0, 0.1),
     'L1_gnn_bo': (0.0, 0.1),
     'L1_gnn_gamma': (1.0, 0.2),
     'L1_gnn_beta': (0.0, 0.1)}
    factors = {}
    for name, (base, spread) in spreads.items():
        noise = np.random.default_rng([zlib.crc32(name.encode()), seed]).standard_normal(out[name].shape)
        drawn = base * np.exp(spread * noise) if base else spread * noise
        out[name] = jnp.asarray(drawn.astype(out[name].dtype))
    for name, factor in factors.items():
        out[name] = (out[name] * factor).astype(out[name].dtype)
    return out
```

```python
import concourse.bass as bass
from concourse import mybir
from contextlib import ExitStack

GRAPHS, NODES, D = 64, 128, 256
HEADS = 8
HD = D // HEADS
HIDDEN = 4 * D
PER = 4
GROUPS = GRAPHS // PER
TOK = PER * NODES
KT = D // 128
HT = HIDDEN // 128
HPT = 128 // HD
EPS = 1e-5
SCALE0 = 1.0 / float(HD) ** 0.5
SCALE1 = 1.0 / float(D) ** 0.5
MASKED = -1.0e30
CONSTS = 5
LN_STEPS = 14


def build(nc, x, adj, ln1_g, ln1_b, ln2_g, ln2_b, wq, bq, wk, bk, wv, bv, wo, bo, w1, b1, w2, b2,
          wq1, wk1, wv1, wo1, bo1, gamma, beta, out):
    f32, i32 = mybir.dt.float32, mybir.dt.int32
    ALU, ACT, AX = mybir.AluOpType, mybir.ActivationFunctionType, mybir.AxisListType

    x_v = x.rearrange("(g b) n d -> g n b d", b=PER)
    adj_v = adj.rearrange("(g b) q k -> g q b k", b=PER)
    out_v = out.rearrange("(g b) n d -> g n b d", b=PER)

    with ExitStack() as ctx:
        def sb(name, shape, dt=f32):
            return ctx.enter_context(nc.sbuf_tensor(name, shape, dt))

        def sem(name):
            return ctx.enter_context(nc.semaphore(name))

        wq_s, wk_s, wv_s, wo_s = (sb(n, [128, KT, D]) for n in ("wq_s", "wk_s", "wv_s", "wo_s"))
        w1_s = sb("w1_s", [128, KT, HIDDEN])
        w2_s = sb("w2_s", [128, HT, D])
        l1_raw = {n: sb(n + "_raw", [128, KT, D]) for n in ("wq1", "wk1", "wv1")}
        l1_T = {n: sb(n + "_T", [128, KT, D]) for n in ("wq1", "wk1", "wv1")}
        wo1_s = sb("wo1_s", [128, KT, D])
        qk1 = sb("qk1", [128, KT, D])
        vo1 = sb("vo1", [128, KT, D])
        cols = {n: sb(n + "_c", [128, KT]) for n in ("ln1_g", "ln1_b", "ln2_g", "ln2_b", "bq", "bk")}
        bqs = sb("bqs", [128, KT])
        b1_c = sb("b1_c", [128, HT])
        rows = {n: sb(n + "_r", [128, D]) for n in ("bv", "bo", "b2", "bo1", "gamma", "beta")}
        ident = sb("ident", [128, 128])
        minus_half = sb("minus_half", [128, PER])

        xs = sb("xs", [128, PER, D])
        adj_i = sb("adj_i", [128, PER, NODES], i32)
        adj_f = sb("adj_f", [128, PER, NODES])
        tenth = sb("tenth", [128, PER, NODES])
        bias0 = sb("bias0", [128, PER, NODES])
        pen0 = sb("pen0", [128, PER, NODES])
        pen1 = sb("pen1", [128, PER, NODES])
        x_bo = sb("x_bo", [128, PER, D])
        nx = sb("nx", [128, PER, D])
        nxT = sb("nxT", [128, KT, TOK])
        qT = sb("qT", [128, KT, TOK])
        k_diag = sb("k_diag", [128, KT, HPT, TOK])
        v_one = sb("v_one", [128, PER, HEADS, HD + 1])
        neg_s = sb("neg_s", [128, 2, HEADS, NODES])
        neg_max = sb("neg_max", [128, 2, HEADS])
        p_s = sb("p_s", [128, 2, HEADS, NODES])
        pT = sb("pT", [128, 2, HEADS, NODES])
        rsum = sb("rsum", [128, 2, HEADS])
        attn = sb("attn", [128, 2, D])
        attnT = sb("attnT", [128, 2, KT, NODES])
        x1 = sb("x1", [128, PER, D])
        n2 = sb("n2", [128, PER, D])
        x1_b2 = sb("x1_b2", [128, PER, D])
        n2T = sb("n2T", [128, KT, TOK])
        hT = sb("hT", [128, HT, TOK])
        x2 = sb("x2", [128, PER, D])
        x2_bo = sb("x2_bo", [128, PER, D])
        x2T = sb("x2T", [128, KT, TOK])
        tT = sb("tT", [128, KT, TOK])
        vo = sb("vo", [128, PER, D])
        neg_s1 = sb("neg_s1", [128, PER, NODES])
        neg_max1 = sb("neg_max1", [128, PER])
        p1 = sb("p1", [128, PER, NODES])
        sum1 = sb("sum1", [128, PER])
        rsum1 = sb("rsum1", [128, PER])
        p1T = sb("p1T", [128, PER, NODES])
        y = sb("y", [128, PER, D])
        n3 = sb("n3", [128, PER, D])
        n3g = sb("n3g", [128, PER, D])
        outs = sb("outs", [128, PER, D])
        lns = {n: dict(stats=sb(f"stats{n}", [128, PER, 6]), mv=sb(f"mv{n}", [128, PER, 2]),
                       ve=sb(f"ve{n}", [128, PER]), rstd=sb(f"rstd{n}", [128, PER]),
                       shift=sb(f"shift{n}", [128, PER])) for n in (1, 2, 3)}

        bank = [ctx.enter_context(nc.psum_tensor(f"bank{i}", [128, 512], f32)) for i in range(8)]

        w_load = sem("w_load")
        x_load = sem("x_load")
        adj_load = sem("adj_load")
        out_store = sem("out_store")
        consts = sem("consts")
        prep_pe = sem("prep_pe")
        prep_dve = sem("prep_dve")
        stand_dve, stand_pool = sem("stand_dve"), sem("stand_pool")
        pe_nxT = sem("pe_nxT")
        pe_k, pe_q, pe_v = sem("pe_k"), sem("pe_q"), sem("pe_v")
        pe_s, pe_pT, pe_av = sem("pe_s"), sem("pe_pT"), sem("pe_av")
        pe_attnT, pe_wo = sem("pe_attnT"), sem("pe_wo")
        pe_n2T = sem("pe_n2T")
        pe_up = sem("pe_up")
        pe_down = sem("pe_down")
        pe_x2T = sem("pe_x2T")
        pe_t, pe_vo = sem("pe_t"), sem("pe_vo")
        pe_s1, pe_p1T = sem("pe_s1"), sem("pe_p1T")
        pe_av1 = sem("pe_av1")
        act_nxT, act_k = sem("act_nxT"), sem("act_k")
        act_q = sem("act_q")
        act_p = sem("act_p")
        act_pT, act_attnT = sem("act_pT"), sem("act_attnT")
        act_n2T = sem("act_n2T")
        act_h = sem("act_h")
        act_x2T, act_t, act_vo = sem("act_x2T"), sem("act_t"), sem("act_vo")
        act_p1 = sem("act_p1")
        ln_dve = {n: sem(f"ln{n}_dve") for n in (1, 2, 3)}
        dve_nxT, dve_k = sem("dve_nxT"), sem("dve_k")
        dve_v = sem("dve_v")
        dve_s = sem("dve_s")
        dve_pT, dve_r, dve_attn = sem("dve_pT"), sem("dve_r"), sem("dve_attn")
        dve_x1 = sem("dve_x1")
        dve_n2T = sem("dve_n2T")
        dve_x2 = sem("dve_x2")
        dve_x2T, dve_t, dve_vo = sem("dve_x2T"), sem("dve_t"), sem("dve_vo")
        dve_s1 = sem("dve_s1")
        dve_p1T, dve_r1 = sem("dve_p1T"), sem("dve_r1")
        dve_y = sem("dve_y")
        ln_pool = {n: sem(f"ln{n}_pool") for n in (1, 2, 3)}
        pool_adj = sem("pool_adj")
        pool_bias = sem("pool_bias")
        pool_pen1 = sem("pool_pen1")
        pool_xbo, pool_x1b, pool_x2b = sem("pool_xbo"), sem("pool_x1b"), sem("pool_x2b")
        pool_out = sem("pool_out")

        weight_loads = [(wq_s, wq), (wk_s, wk), (wv_s, wv), (wo_s, wo), (w1_s, w1), (w2_s, w2),
                        (l1_raw["wq1"], wq1), (l1_raw["wk1"], wk1), (l1_raw["wv1"], wv1), (wo1_s, wo1)]
        col_loads = [(cols["ln1_g"], ln1_g), (cols["ln1_b"], ln1_b), (cols["ln2_g"], ln2_g),
                     (cols["ln2_b"], ln2_b), (cols["bq"], bq), (cols["bk"], bk), (b1_c, b1)]
        row_loads = [(rows["bv"], bv), (rows["bo"], bo), (rows["b2"], b2), (rows["bo1"], bo1),
                     (rows["gamma"], gamma), (rows["beta"], beta)]
        W_ALL = 16 * (len(weight_loads) + len(col_loads) + len(row_loads))

        block = ctx.enter_context(nc.Block())

        @block.sync
        def _(sp):
            def load(g):
                sp.wait_ge(ln_dve[1], LN_STEPS * g)
                sp.wait_ge(pool_xbo, g)
                sp.dma_start(xs[:, :, :], x_v[g]).then_inc(x_load, 16)
                sp.wait_ge(pool_adj, g)
                sp.dma_start(adj_i[:, :, :], adj_v[g]).then_inc(adj_load, 16)

            def store(g):
                sp.wait_ge(pool_out, 2 * g + 2)
                sp.dma_start(out_v[g], outs[:, :, :]).then_inc(out_store, 16)

            load(0)
            for dst, src in weight_loads:
                sp.dma_start(dst[:, :, :], src.rearrange("(t p) n -> p t n", p=128)).then_inc(w_load, 16)
            load(1)
            load(2)
            store(0)
            with sp.Fori(2, GROUPS - 1) as g:
                load(g + 1)
                store(g - 1)
            store(GROUPS - 2)
            store(GROUPS - 1)
            sp.wait_ge(out_store, 16 * GROUPS)

        @block.tensor
        def _(pe):
            mm, tr = nc.tensor.matmul, nc.tensor.transpose

            pe.wait_ge(w_load, W_ALL)
            pe.wait_ge(consts, CONSTS)
            for i, n in enumerate(("wq1", "wk1", "wv1")):
                for c in range(KT):
                    for r in range(KT):
                        last = tr(bank[2 * i + c][:, 128 * r:128 * r + 128],
                                  l1_raw[n][:, r, 128 * c:128 * c + 128], ident[:, :])
                last.then_inc(prep_pe, 1)
            pe.wait_ge(prep_dve, 3)
            for m in range(KT):
                for c in range(KT):
                    last = mm(bank[6][:, 256 * m:256 * m + 256], l1_T["wq1"][:, c, 128 * m:128 * m + 128],
                              l1_T["wk1"][:, c, :], start=(c == 0), stop=(c == KT - 1))
            last.then_inc(prep_pe, 1)
            for m in range(KT):
                for c in range(KT):
                    last = mm(bank[7][:, 256 * m:256 * m + 256], l1_T["wv1"][:, c, 128 * m:128 * m + 128],
                              wo1_s[:, c, :], start=(c == 0), stop=(c == KT - 1))
            last.then_inc(prep_pe, 1)
            pe.wait_ge(prep_dve, 5)

            def nodes(b):
                return slice(128 * b, 128 * b + 128)

            def norm_transpose(g):
                pe.wait_ge(ln_dve[1], LN_STEPS * g + LN_STEPS)
                pe.wait_ge(act_pT, 4 * g)
                pe.wait_ge(dve_pT, 4 * g)
                for t in range(KT):
                    for b in range(PER):
                        last = tr(bank[2 + t][:, nodes(b)], nx[:, b, 128 * t:128 * t + 128], ident[:, :])
                last.then_inc(pe_nxT, 1)

            def project(g):
                pe.wait_ge(act_nxT, g + 1)
                pe.wait_ge(dve_nxT, g + 1)
                for m in range(KT):
                    for t in range(KT):
                        last = mm(bank[2 + m][:, :], wk_s[:, t, 128 * m:128 * m + 128], nxT[:, t, :],
                                  start=(t == 0), stop=(t == KT - 1))
                    last.then_inc(pe_k, 1)
                pe.wait_ge(dve_s, 4 * g)
                for m in range(KT):
                    for t in range(KT):
                        last = mm(bank[m][:, :], wq_s[:, t, 128 * m:128 * m + 128], nxT[:, t, :],
                                  start=(t == 0), stop=(t == KT - 1))
                    last.then_inc(pe_q, 1)
                pe.wait_ge(dve_attn, 4 * g)
                pe.wait_ge(dve_x1, 4 * g)
                for half in range(2):
                    for b in (2 * half, 2 * half + 1):
                        for t in range(KT):
                            last = mm(bank[4 + half][:, 256 * (b % 2):256 * (b % 2) + 256],
                                      nxT[:, t, nodes(b)], wv_s[:, t, :], start=(t == 0), stop=(t == KT - 1))
                    last.then_inc(pe_v, 1)

            def scores(g, b):
                if b == 0:
                    pe.wait_ge(act_q, 2 * g + 2)
                    pe.wait_ge(act_k, 4 * g + 4)
                    pe.wait_ge(dve_k, 4 * g + 4)
                else:
                    pe.wait_ge(dve_s, 4 * g + b)
                for t in range(KT):
                    last = mm(bank[t][:, :], qT[:, t, nodes(b)], k_diag[:, t, :, nodes(b)], start=True, stop=True)
                last.then_inc(pe_s, 1)

            def p_transpose(g, b):
                pe.wait_ge(act_p, 4 * g + b + 1)
                if b > 0:
                    pe.wait_ge(act_pT, 4 * g + b)
                    pe.wait_ge(dve_pT, 4 * g + b)
                for h in range(HEADS):
                    last = tr(bank[2 + h // HPT][:, nodes(h % HPT)], p_s[:, b % 2, h, :], ident[:, :])
                last.then_inc(pe_pT, 1)

            def attend(g, b):
                pe.wait_ge(act_pT, 4 * g + b + 1)
                pe.wait_ge(dve_pT, 4 * g + b + 1)
                pe.wait_ge(dve_v, 2 * g + 2)
                pe.wait_ge(dve_attn, 4 * g + b)
                for h in range(HEADS):
                    last = mm(bank[4][:, (HD + 1) * h:(HD + 1) * (h + 1)], pT[:, b % 2, h, :],
                              v_one[:, b, h, :], start=True, stop=True)
                last.then_inc(pe_av, 1)

            def attn_transpose(g, b):
                pe.wait_ge(dve_attn, 4 * g + b + 1)
                pe.wait_ge(dve_x1, 4 * g + b)
                for t in range(KT):
                    last = tr(bank[5][:, nodes(t)], attn[:, b % 2, 128 * t:128 * t + 128], ident[:, :])
                last.then_inc(pe_attnT, 1)

            def out_project(g, b):
                pe.wait_ge(act_attnT, 4 * g + b + 1)
                for t in range(KT):
                    last = mm(bank[5][:, 0:D], attnT[:, b % 2, t, :], wo_s[:, t, :], start=(t == 0), stop=(t == KT - 1))
                last.then_inc(pe_wo, 1)

            def n2_transpose(g):
                pe.wait_ge(ln_dve[2], LN_STEPS * g + LN_STEPS)
                pe.wait_ge(dve_y, 4 * g)
                for t in range(KT):
                    for b in range(PER):
                        last = tr(bank[6 + t][:, nodes(b)], n2[:, b, 128 * t:128 * t + 128], ident[:, :])
                last.then_inc(pe_n2T, 1)

            def mlp_up(g, j):
                if j == 0:
                    pe.wait_ge(act_n2T, g + 1)
                    pe.wait_ge(dve_n2T, g + 1)
                elif j >= 2:
                    pe.wait_ge(act_h, HT * g + j - 1)
                for t in range(KT):
                    last = mm(bank[6 + j % 2][:, :], w1_s[:, t, 128 * j:128 * j + 128], n2T[:, t, :],
                              start=(t == 0), stop=(t == KT - 1))
                last.then_inc(pe_up, 1)

            def mlp_down(g, b):
                pe.wait_ge(act_h, HT * g + HT)
                if b >= 2:
                    pe.wait_ge(dve_x2, 4 * g + b - 1)
                for j in range(HT):
                    last = mm(bank[6 + b % 2][:, 0:D], hT[:, j, nodes(b)], w2_s[:, j, :],
                              start=(j == 0), stop=(j == HT - 1))
                last.then_inc(pe_down, 1)

            def x2_transpose(g):
                pe.wait_ge(dve_x2, 4 * g + 4)
                for t in range(KT):
                    for b in range(PER):
                        last = tr(bank[6 + t][:, nodes(b)], x2[:, b, 128 * t:128 * t + 128], ident[:, :])
                last.then_inc(pe_x2T, 1)

            def t_project(g):
                pe.wait_ge(act_x2T, g + 1)
                pe.wait_ge(dve_x2T, g + 1)
                for m in range(KT):
                    for t in range(KT):
                        last = mm(bank[6 + m][:, :], qk1[:, t, 128 * m:128 * m + 128], x2T[:, t, :],
                                  start=(t == 0), stop=(t == KT - 1))
                    last.then_inc(pe_t, 1)

            def scores1(g):
                pe.wait_ge(act_t, g + 1)
                pe.wait_ge(dve_t, g + 1)
                for b in range(PER):
                    for t in range(KT):
                        last = mm(bank[6][:, nodes(b)], tT[:, t, nodes(b)], x2T[:, t, nodes(b)],
                                  start=(t == 0), stop=(t == KT - 1))
                last.then_inc(pe_s1, 1)

            def vo_project(g, half):
                if half == 1:
                    pe.wait_ge(dve_s1, g + 1)
                for b in (2 * half, 2 * half + 1):
                    for t in range(KT):
                        last = mm(bank[7 - half][:, 256 * (b % 2):256 * (b % 2) + 256], x2T[:, t, nodes(b)],
                                  vo1[:, t, :], start=(t == 0), stop=(t == KT - 1))
                last.then_inc(pe_vo, 1)

            def p1_transpose(g):
                pe.wait_ge(act_p1, 4 * g + 4)
                pe.wait_ge(act_vo, g + 1)
                for b in range(PER):
                    last = tr(bank[7][:, nodes(b)], p1[:, b, :], ident[:, :])
                last.then_inc(pe_p1T, 1)

            def attend1(g):
                pe.wait_ge(dve_p1T, g + 1)
                pe.wait_ge(dve_vo, g + 1)
                for half in range(2):
                    for b in (2 * half, 2 * half + 1):
                        last = mm(bank[6 + half][:, 256 * (b % 2):256 * (b % 2) + 256], p1T[:, b, :], vo[:, b, :],
                                  start=True, stop=True)
                    last.then_inc(pe_av1, 1)

            def turn(ga, gb):
                A, B = ga is not None, gb is not None
                if B:
                    n2_transpose(gb)
                    for j in range(HT // 2):
                        mlp_up(gb, j)
                if A:
                    norm_transpose(ga)
                if B:
                    for j in range(HT // 2, HT):
                        mlp_up(gb, j)
                if A:
                    project(ga)
                for k in range(PER + 1):
                    if A and k < PER:
                        scores(ga, k)
                    if A and k >= 1:
                        p_transpose(ga, k - 1)
                    if A and k >= 2:
                        attn_transpose(ga, k - 2)
                    if B and k < PER:
                        mlp_down(gb, k)
                    if B and k == PER:
                        x2_transpose(gb)
                    if A and k >= 1:
                        attend(ga, k - 1)
                    if A and k >= 2:
                        out_project(ga, k - 2)
                if B:
                    t_project(gb)
                if A:
                    attn_transpose(ga, PER - 1)
                if B:
                    scores1(gb)
                if A:
                    out_project(ga, PER - 1)
                if B:
                    vo_project(gb, 0)
                    vo_project(gb, 1)
                    p1_transpose(gb)
                    attend1(gb)

            turn(0, None)
            turn(1, 0)
            with pe.Fori(2, GROUPS) as g:
                turn(g, g - 1)
            turn(None, GROUPS - 1)

        @block.scalar
        def _(act):
            run = nc.scalar.activation
            for dst, src in col_loads:
                with nc.allow_non_contiguous_dma(reason="a bias vector onto partitions"):
                    act.dma_start(dst[:, :], src.rearrange("(t p) -> p t", p=128)).then_inc(w_load, 16)
            for dst, src in row_loads:
                act.dma_start(dst[:, :], src.rearrange("(a d) -> a d", a=1).to_broadcast([128, D])).then_inc(w_load, 16)
            act.wait_ge(w_load, W_ALL)
            act.wait_ge(prep_dve, 6)
            act.wait_ge(consts, CONSTS)

            def nxT_copy(g):
                act.wait_ge(pe_nxT, g + 1)
                act.wait_ge(pe_v, 2 * g)
                run(nxT[:, 0, :], bank[2][:, :], ACT.Identity, scale=cols["ln1_g"][:, 0:1],
                    bias=cols["ln1_b"][:, 0:1]).then_inc(act_nxT, 1)

            def k_copy(g):
                act.wait_ge(pe_k, 2 * g + 1)
                act.wait_ge(pe_s, 4 * g)
                for r in range(HPT):
                    s = slice(HD * r, HD * r + HD)
                    run(k_diag[s, 0, r, :], bank[2][s, :], ACT.Identity, bias=cols["bk"][s, 0:1]).then_inc(act_k, 1)

            def q_copy(g):
                for t in range(KT):
                    act.wait_ge(pe_q, 2 * g + t + 1)
                    run(qT[:, t, :], bank[t][:, :], ACT.Identity, scale=SCALE0, bias=bqs[:, t:t + 1]).then_inc(act_q, 1)

            def exps(g, b):
                act.wait_ge(dve_s, 4 * g + b + 1)
                act.wait_ge(pe_pT, 4 * g + max(b - 1, 0))
                for h in range(HEADS):
                    last = run(p_s[:, b % 2, h, :], neg_s[:, b % 2, h, :], ACT.Exp, scale=-1.0,
                               bias=neg_max[:, b % 2, h:h + 1])
                last.then_inc(act_p, 1)

            def pT_copy(g, b):
                act.wait_ge(pe_pT, 4 * g + b + 1)
                act.wait_ge(pe_av, 4 * g + max(b - 1, 0))
                run(pT[:, b % 2, 0:HPT, :], bank[2][:, :].rearrange("p (h n) -> p h n", h=HPT),
                    ACT.Identity).then_inc(act_pT, 1)

            def attnT_copy(g, b):
                act.wait_ge(pe_attnT, 4 * g + b + 1)
                act.wait_ge(pe_wo, 4 * g + max(b - 1, 0))
                run(attnT[:, b % 2, :, :], bank[5][:, 0:D].rearrange("p (t n) -> p t n", t=KT),
                    ACT.Identity).then_inc(act_attnT, 1)

            def n2T_copy(g):
                act.wait_ge(pe_n2T, g + 1)
                act.wait_ge(pe_up, HT * g)
                run(n2T[:, 0, :], bank[6][:, :], ACT.Identity, scale=cols["ln2_g"][:, 0:1],
                    bias=cols["ln2_b"][:, 0:1]).then_inc(act_n2T, 1)

            def gelu(g, j):
                act.wait_ge(pe_up, HT * g + j + 1)
                if j == 0:
                    act.wait_ge(pe_down, 4 * g)
                run(hT[:, j, :], bank[6 + j % 2][:, :], ACT.Gelu, bias=b1_c[:, j:j + 1]).then_inc(act_h, 1)

            def x2T_copy(g):
                act.wait_ge(pe_x2T, g + 1)
                act.wait_ge(pe_vo, 2 * g)
                run(x2T[:, 0, :], bank[6][:, :], ACT.Identity).then_inc(act_x2T, 1)

            def t_copy(g):
                act.wait_ge(pe_t, 2 * g + 1)
                act.wait_ge(pe_s1, g)
                run(tT[:, 0, :], bank[6][:, :], ACT.Identity).then_inc(act_t, 1)

            def exps1(g):
                act.wait_ge(dve_s1, g + 1)
                act.wait_ge(pe_p1T, g)
                act.wait_ge(dve_r1, g)
                for b in range(PER):
                    run(p1[:, b, :], neg_s1[:, b, :], ACT.Exp, scale=-1.0, bias=neg_max1[:, b:b + 1],
                        accum_out=sum1[:, b:b + 1]).then_inc(act_p1, 1)

            def vo_copy(g):
                act.wait_ge(pe_vo, 2 * g + 1)
                act.wait_ge(pe_av1, 2 * g)
                run(vo[:, 0:2, :], bank[7][:, :].rearrange("p (b d) -> p b d", b=2), ACT.Identity).then_inc(act_vo, 1)

            def turn(ga, gb):
                A, B = ga is not None, gb is not None
                if B:
                    n2T_copy(gb)
                    for j in range(HT // 2):
                        gelu(gb, j)
                if A:
                    nxT_copy(ga)
                if B:
                    for j in range(HT // 2, HT):
                        gelu(gb, j)
                if A:
                    k_copy(ga)
                    q_copy(ga)
                for k in range(PER + 1):
                    if A and k >= 1:
                        pT_copy(ga, k - 1)
                    if A and k >= 2:
                        attnT_copy(ga, k - 2)
                    if A and k < PER:
                        exps(ga, k)
                if B:
                    x2T_copy(gb)
                    t_copy(gb)
                if A:
                    attnT_copy(ga, PER - 1)
                if B:
                    exps1(gb)
                    vo_copy(gb)

            turn(0, None)
            turn(1, 0)
            with act.Fori(2, GROUPS) as g:
                turn(g, g - 1)
            turn(None, GROUPS - 1)

        @block.vector
        def _(dve):
            V = nc.vector
            V.memset(v_one[:, :, :, :], 1.0).then_inc(consts, 1)
            V.memset(minus_half[:, :], -0.5).then_inc(consts, 1)
            for i, n in enumerate(("wq1", "wk1", "wv1")):
                dve.wait_ge(prep_pe, i + 1)
                for c in range(KT):
                    last = V.tensor_copy(l1_T[n][:, c, :], bank[2 * i + c][:, 0:D])
                last.then_inc(prep_dve, 1)
            dve.wait_ge(prep_pe, 4)
            V.tensor_scalar(qk1[:, :, :], bank[6][:, :].rearrange("p (m d) -> p m d", m=KT), SCALE1, None,
                            ALU.mult).then_inc(prep_dve, 1)
            dve.wait_ge(prep_pe, 5)
            V.tensor_copy(vo1[:, :, :], bank[7][:, :].rearrange("p (m d) -> p m d", m=KT)).then_inc(prep_dve, 1)
            dve.wait_ge(w_load, W_ALL)
            V.tensor_scalar(bqs[:, :], cols["bq"][:, :], SCALE0, None, ALU.mult).then_inc(prep_dve, 1)
            dve.wait_ge(consts, CONSTS)

            def layer_norm(n, g, src, dst):
                t, s, base = lns[n], ln_dve[n], LN_STEPS * g
                for b in range(PER):
                    V.bn_stats(t["stats"][:, b, :], src[:, b, :]).then_inc(s, 1)
                dve.wait_ge(s, base + 4)
                dve.sem_inc(stand_dve, 1)
                for b in range(PER):
                    V.bn_aggr(t["mv"][:, b, :], t["stats"][:, b, :]).then_inc(s, 1)
                dve.wait_ge(s, base + 8)
                dve.wait_ge(ln_pool[n], g)
                V.tensor_scalar(t["ve"][:, :], t["mv"][:, :, 1], EPS, None, ALU.add).then_inc(s, 1)
                dve.wait_ge(ln_pool[n], g + 1)
                V.scalar_tensor_tensor(out=t["shift"][:, :], in0=t["mv"][:, :, 0], scalar=-1.0, in1=t["rstd"][:, :],
                                       op0=ALU.mult, op1=ALU.mult).then_inc(s, 1)
                dve.wait_ge(s, base + 10)
                for b in range(PER):
                    V.tensor_scalar(dst[:, b, :], src[:, b, :], t["rstd"][:, b:b + 1], t["shift"][:, b:b + 1],
                                    ALU.mult, ALU.add).then_inc(s, 1)

            def norm1(g):
                dve.wait_ge(x_load, 16 * g + 16)
                dve.wait_ge(pe_nxT, g)
                layer_norm(1, g, xs, nx)

            def nxT_copy(g):
                dve.wait_ge(pe_nxT, g + 1)
                dve.wait_ge(pe_v, 2 * g)
                V.tensor_scalar(nxT[:, 1, :], bank[3][:, :], cols["ln1_g"][:, 1:2], cols["ln1_b"][:, 1:2],
                                ALU.mult, ALU.add).then_inc(dve_nxT, 1)

            def k_copy(g):
                dve.wait_ge(pe_k, 2 * g + 2)
                dve.wait_ge(pe_s, 4 * g)
                for r in range(HPT):
                    s = slice(HD * r, HD * r + HD)
                    V.tensor_scalar(k_diag[s, 1, r, :], bank[3][s, :], cols["bk"][s, 1:2], None,
                                    ALU.add).then_inc(dve_k, 1)

            def v_copy(g):
                dve.wait_ge(pe_av, 4 * g)
                for half in range(2):
                    dve.wait_ge(pe_v, 2 * g + half + 1)
                    for i in range(2):
                        last = V.tensor_tensor(v_one[:, 2 * half + i, :, 0:HD],
                                               bank[4 + half][:, D * i:D * i + D].rearrange("p (h d) -> p h d", h=HEADS),
                                               rows["bv"][:, :].rearrange("p (h d) -> p h d", h=HEADS), ALU.add)
                    last.then_inc(dve_v, 1)

            def biased(g, b):
                dve.wait_ge(pe_s, 4 * g + b + 1)
                if b == 0:
                    dve.wait_ge(pool_bias, 4 * g + 4)
                dve.wait_ge(act_p, 4 * g + max(b - 1, 0))
                dve.sem_inc(stand_dve, 1)
                for h in range(HEADS):
                    last = V.tensor_tensor_reduce(neg_s[:, b % 2, h, :], bank[h // HPT][:, NODES * (h % HPT):NODES * (h % HPT) + NODES],
                                                  bias0[:, b, :], -1.0, -3.0 * MASKED, ALU.add, ALU.min,
                                                  neg_max[:, b % 2, h:h + 1])
                last.then_inc(dve_s, 1)

            def pT_copy(g, b):
                dve.wait_ge(pe_pT, 4 * g + b + 1)
                dve.wait_ge(pe_av, 4 * g + max(b - 1, 0))
                V.tensor_copy(pT[:, b % 2, HPT:HEADS, :],
                              bank[3][:, :].rearrange("p (h n) -> p h n", h=HPT)).then_inc(dve_pT, 1)

            def normalise(g, b):
                dve.wait_ge(pe_av, 4 * g + b + 1)
                dve.wait_ge(pe_attnT, 4 * g + max(b - 1, 0))
                av = bank[4][:, 0:HEADS * (HD + 1)].rearrange("p (h d) -> p h d", h=HEADS)
                V.reciprocal(rsum[:, b % 2, :], av[:, :, HD]).then_inc(dve_r, 1)
                dve.wait_ge(dve_r, 4 * g + b + 1)
                V.tensor_tensor(attn[:, b % 2, :].rearrange("p (h d) -> p h d", h=HEADS), av[:, :, 0:HD],
                                rsum[:, b % 2, :, None].to_broadcast([128, HEADS, HD]), ALU.mult).then_inc(dve_attn, 1)

            def residual1(g, b):
                dve.wait_ge(pe_wo, 4 * g + b + 1)
                if b == 0:
                    dve.wait_ge(pool_xbo, g + 1)
                    dve.wait_ge(pool_x1b, g)
                V.tensor_tensor(x1[:, b, :], bank[5][:, 0:D], x_bo[:, b, :], ALU.add).then_inc(dve_x1, 1)

            def norm2(g):
                dve.wait_ge(dve_x1, 4 * g + 4)
                dve.wait_ge(pe_n2T, g)
                layer_norm(2, g, x1, n2)

            def n2T_copy(g):
                dve.wait_ge(pe_n2T, g + 1)
                dve.wait_ge(pe_up, HT * g)
                V.tensor_scalar(n2T[:, 1, :], bank[7][:, :], cols["ln2_g"][:, 1:2], cols["ln2_b"][:, 1:2],
                                ALU.mult, ALU.add).then_inc(dve_n2T, 1)

            def residual2(g, b):
                dve.wait_ge(pe_down, 4 * g + b + 1)
                if b == 0:
                    dve.wait_ge(pool_x1b, g + 1)
                    dve.wait_ge(pool_x2b, g)
                    dve.wait_ge(pe_x2T, g)
                V.tensor_tensor(x2[:, b, :], bank[6 + b % 2][:, 0:D], x1_b2[:, b, :], ALU.add).then_inc(dve_x2, 1)

            def x2T_copy(g):
                dve.wait_ge(pe_x2T, g + 1)
                dve.wait_ge(pe_vo, 2 * g)
                V.tensor_copy(x2T[:, 1, :], bank[7][:, :]).then_inc(dve_x2T, 1)

            def t_copy(g):
                dve.wait_ge(pe_t, 2 * g + 2)
                dve.wait_ge(pe_s1, g)
                V.tensor_copy(tT[:, 1, :], bank[7][:, :]).then_inc(dve_t, 1)

            def biased1(g):
                dve.wait_ge(pe_s1, g + 1)
                dve.wait_ge(pool_pen1, g + 1)
                dve.wait_ge(act_p1, 4 * g)
                dve.sem_inc(stand_dve, 1)
                for b in range(PER):
                    last = V.tensor_tensor_reduce(neg_s1[:, b, :], bank[6][:, NODES * b:NODES * b + NODES],
                                                  pen1[:, b, :], -1.0, -3.0 * MASKED, ALU.add, ALU.min, neg_max1[:, b:b + 1])
                last.then_inc(dve_s1, 1)

            def vo_copy(g):
                dve.wait_ge(pe_vo, 2 * g + 2)
                dve.wait_ge(pe_av1, 2 * g)
                V.tensor_copy(vo[:, 2:4, :], bank[6][:, :].rearrange("p (b d) -> p b d", b=2)).then_inc(dve_vo, 1)

            def p1T_copy(g):
                dve.wait_ge(pe_p1T, g + 1)
                dve.wait_ge(pe_av1, 2 * g)
                V.tensor_copy(p1T[:, :, :], bank[7][:, :].rearrange("p (b n) -> p b n", b=PER)).then_inc(dve_p1T, 1)
                dve.wait_ge(act_p1, 4 * g + 4)
                V.reciprocal(rsum1[:, :], sum1[:, :]).then_inc(dve_r1, 1)

            def residual3(g):
                dve.wait_ge(dve_r1, g + 1)
                dve.wait_ge(pool_x2b, g + 1)
                for b in range(PER):
                    if b % 2 == 0:
                        dve.wait_ge(pe_av1, 2 * g + b // 2 + 1)
                    V.scalar_tensor_tensor(out=y[:, b, :], in0=bank[6 + b // 2][:, D * (b % 2):D * (b % 2) + D],
                                           scalar=rsum1[:, b:b + 1], in1=x2_bo[:, b, :],
                                           op0=ALU.mult, op1=ALU.add).then_inc(dve_y, 1)

            def norm3(g):
                dve.wait_ge(dve_y, 4 * g + 4)
                dve.wait_ge(pool_out, 2 * g)
                layer_norm(3, g, y, n3)

            def turn(ga, gb):
                A, B = ga is not None, gb is not None
                if B:
                    n2T_copy(gb)
                if A:
                    norm1(ga)
                    nxT_copy(ga)
                    k_copy(ga)
                    v_copy(ga)
                for k in range(PER + 1):
                    if A and k < PER:
                        biased(ga, k)
                    if A and k >= 1:
                        pT_copy(ga, k - 1)
                    if B and k < PER:
                        residual2(gb, k)
                    if B and k == PER:
                        x2T_copy(gb)
                    if A and k >= 1:
                        normalise(ga, k - 1)
                    if A and k >= 2:
                        residual1(ga, k - 2)
                if B:
                    t_copy(gb)
                    biased1(gb)
                if A:
                    residual1(ga, PER - 1)
                    norm2(ga)
                if B:
                    vo_copy(gb)
                    p1T_copy(gb)
                    residual3(gb)
                    norm3(gb)

            turn(0, None)
            turn(1, 0)
            with dve.Fori(2, GROUPS) as g:
                turn(g, g - 1)
            turn(None, GROUPS - 1)

        @block.gpsimd
        def _(pool):
            P = nc.gpsimd
            P.memset(k_diag[:, :, :, :], 0.0).then_inc(consts, 1)
            P.memset(ident[:, :], 0.0).then_inc(consts, 1)
            pool.wait_ge(consts, 4)
            P.affine_select(out=ident[:, :], in_=ident[:, :], compare_op=ALU.not_equal, fill=1.0, base=0,
                            pattern=[[-1, 128]], channel_multiplier=1).then_inc(consts, 1)
            pool.wait_ge(w_load, W_ALL)

            def rstd(n, g):
                pool.wait_ge(ln_dve[n], LN_STEPS * g + 9)
                P.tensor_tensor(lns[n]["rstd"][:, :], lns[n]["ve"][:, :], minus_half[:, :], ALU.pow).then_inc(ln_pool[n], 1)

            def bias(g):
                pool.wait_ge(adj_load, 16 * g + 16)
                pool.wait_ge(pool_pen1, g)
                pool.sem_inc(stand_pool, 1)
                P.tensor_copy(adj_f[:, :, :], adj_i[:, :, :]).then_inc(pool_adj, 1)
                pool.wait_ge(pool_adj, g + 1)
                pool.sem_inc(stand_pool, 1)
                P.tensor_scalar(tenth[:, :, :], adj_f[:, :, :], 0.1, None, ALU.mult).then_inc(pool_bias, 1)
                P.tensor_scalar(pen0[:, :, :], adj_f[:, :, :], 0.0, MASKED, ALU.is_le, ALU.mult).then_inc(pool_bias, 1)
                pool.wait_ge(dve_s, 4 * g)
                pool.wait_ge(pool_bias, 4 * g + 2)
                P.tensor_tensor(bias0[:, :, :], tenth[:, :, :], adj_f[:, :, :], ALU.mult).then_inc(pool_bias, 1)
                pool.wait_ge(pool_bias, 4 * g + 3)
                P.tensor_tensor(bias0[:, :, :], bias0[:, :, :], pen0[:, :, :], ALU.add).then_inc(pool_bias, 1)

            def x_plus_bo(g):
                pool.wait_ge(x_load, 16 * g + 16)
                pool.wait_ge(dve_x1, 4 * g)
                P.tensor_tensor(x_bo[:, :, :], xs[:, :, :],
                                rows["bo"][:, None, :].to_broadcast([128, PER, D]), ALU.add).then_inc(pool_xbo, 1)

            def mask1(g):
                pool.wait_ge(dve_s1, g)
                pool.sem_inc(stand_pool, 1)
                P.tensor_scalar(pen1[:, :, :], adj_f[:, :, :], 0.0, MASKED, ALU.is_equal, ALU.mult).then_inc(pool_pen1, 1)

            def x1_plus_b2(g):
                pool.wait_ge(dve_x1, 4 * g + 4)
                pool.wait_ge(dve_x2, 4 * g)
                P.tensor_tensor(x1_b2[:, :, :], x1[:, :, :],
                                rows["b2"][:, None, :].to_broadcast([128, PER, D]), ALU.add).then_inc(pool_x1b, 1)

            def x2_plus_bo(g):
                pool.wait_ge(dve_x2, 4 * g + 4)
                pool.wait_ge(dve_y, 4 * g)
                P.tensor_tensor(x2_bo[:, :, :], x2[:, :, :],
                                rows["bo1"][:, None, :].to_broadcast([128, PER, D]), ALU.add).then_inc(pool_x2b, 1)

            def finish(g):
                pool.wait_ge(ln_dve[3], LN_STEPS * g + LN_STEPS)
                P.tensor_tensor(n3g[:, :, :], n3[:, :, :],
                                rows["gamma"][:, None, :].to_broadcast([128, PER, D]), ALU.mult).then_inc(pool_out, 1)
                pool.wait_ge(pool_out, 2 * g + 1)
                pool.wait_ge(out_store, 16 * g)
                P.tensor_tensor(outs[:, :, :], n3g[:, :, :],
                                rows["beta"][:, None, :].to_broadcast([128, PER, D]), ALU.add).then_inc(pool_out, 1)

            def turn(ga, gb):
                A, B = ga is not None, gb is not None
                if A:
                    rstd(1, ga)
                    bias(ga)
                    x_plus_bo(ga)
                if B:
                    x2_plus_bo(gb)
                if A:
                    rstd(2, ga)
                    x1_plus_b2(ga)
                if B:
                    rstd(3, gb)
                if A:
                    mask1(ga)
                if B:
                    finish(gb)

            turn(0, None)
            turn(1, 0)
            with pool.Fori(2, GROUPS) as g:
                turn(g, g - 1)
            turn(None, GROUPS - 1)


_INS = ['x', 'adj', 'L0_gnn_ln1_g', 'L0_gnn_ln1_b', 'L0_gnn_ln2_g', 'L0_gnn_ln2_b', 'L0_gnn_wq', 'L0_gnn_bq',
        'L0_gnn_wk', 'L0_gnn_bk', 'L0_gnn_wv', 'L0_gnn_bv', 'L0_gnn_wo', 'L0_gnn_bo', 'L0_gnn_w1', 'L0_gnn_b1',
        'L0_gnn_w2', 'L0_gnn_b2', 'L1_gnn_Wq', 'L1_gnn_Wk', 'L1_gnn_Wv', 'L1_gnn_Wo', 'L1_gnn_bo',
        'L1_gnn_gamma', 'L1_gnn_beta']


def kernel(**inputs):
    import numpy as _np
    import concourse.bacc as _bacc
    from concourse import mybir as _mybir
    from concourse.bass_utils import run_bass_kernel_spmd as _run

    nc = _bacc.Bacc("TRN2", target_bir_lowering=False, num_devices=1)
    arrays, args = {}, []
    for name in _INS:
        a = _np.ascontiguousarray(inputs[name])
        arrays[f"in_{name}"] = a
        args.append(nc.dram_tensor(f"in_{name}", a.shape, _mybir.dt.from_np(a.dtype), kind="ExternalInput").ap())
    args.append(nc.dram_tensor("out_0", (GRAPHS, NODES, D), _mybir.dt.float32, kind="ExternalOutput").ap())
    build(nc, *args)
    r = _run(nc, [arrays], core_ids=[0])
    return r.results[0]["out_0"]
```

```python
import concourse.bass as bass
from concourse import mybir
from contextlib import ExitStack

GRAPHS, NODES, D = 64, 128, 256
HEADS = 8
HD = D // HEADS
HIDDEN = 4 * D
PER = 4
GROUPS = GRAPHS // PER
TOK = PER * NODES
KT = D // 128
HT = HIDDEN // 128
HPT = 128 // HD
EPS = 1e-5
SCALE0 = 1.0 / float(HD) ** 0.5
SCALE1 = 1.0 / float(D) ** 0.5
MASKED = -1.0e30
CONSTS = 5
LN_STEPS = 14


def build(nc, x, adj, ln1_g, ln1_b, ln2_g, ln2_b, wq, bq, wk, bk, wv, bv, wo, bo, w1, b1, w2, b2,
          wq1, wk1, wv1, wo1, bo1, gamma, beta, out):
    f32, i32 = mybir.dt.float32, mybir.dt.int32
    ALU, ACT, AX = mybir.AluOpType, mybir.ActivationFunctionType, mybir.AxisListType

    x_v = x.rearrange("(g b) n d -> g n b d", b=PER)
    adj_v = adj.rearrange("(g b) q k -> g q b k", b=PER)
    out_v = out.rearrange("(g b) n d -> g n b d", b=PER)

    with ExitStack() as ctx:
        def sb(name, shape, dt=f32):
            return ctx.enter_context(nc.sbuf_tensor(name, shape, dt))

        def sem(name):
            return ctx.enter_context(nc.semaphore(name))

        wq_s, wk_s, wv_s, wo_s = (sb(n, [128, KT, D]) for n in ("wq_s", "wk_s", "wv_s", "wo_s"))
        w1_s = sb("w1_s", [128, KT, HIDDEN])
        w2_s = sb("w2_s", [128, HT, D])
        l1_raw = {n: sb(n + "_raw", [128, KT, D]) for n in ("wq1", "wk1", "wv1")}
        l1_T = {n: sb(n + "_T", [128, KT, D]) for n in ("wq1", "wk1", "wv1")}
        wo1_s = sb("wo1_s", [128, KT, D])
        qk1 = sb("qk1", [128, KT, D])
        vo1 = sb("vo1", [128, KT, D])
        cols = {n: sb(n + "_c", [128, KT]) for n in ("ln1_g", "ln1_b", "ln2_g", "ln2_b", "bq", "bk")}
        bqs = sb("bqs", [128, KT])
        b1_c = sb("b1_c", [128, HT])
        rows = {n: sb(n + "_r", [128, D]) for n in ("bv", "bo", "b2", "bo1", "gamma", "beta")}
        ident = sb("ident", [128, 128])
        minus_half = sb("minus_half", [128, PER])
        gelu_probe = sb("gelu_probe", [128, 1])

        xs = sb("xs", [128, PER, D])
        adj_i = sb("adj_i", [128, PER, NODES], i32)
        adj_f = sb("adj_f", [128, PER, NODES])
        tenth = sb("tenth", [128, PER, NODES])
        bias0 = sb("bias0", [128, PER, NODES])
        pen0 = sb("pen0", [128, PER, NODES])
        pen1 = sb("pen1", [128, PER, NODES])
        x_bo = sb("x_bo", [128, PER, D])
        nx = sb("nx", [128, PER, D])
        nxT = sb("nxT", [128, KT, TOK])
        qT = sb("qT", [128, KT, TOK])
        k_diag = sb("k_diag", [128, KT, HPT, TOK])
        v_one = sb("v_one", [128, PER, HEADS, HD + 1])
        neg_s = sb("neg_s", [128, 2, HEADS, NODES])
        neg_max = sb("neg_max", [128, 2, HEADS])
        p_s = sb("p_s", [128, 2, HEADS, NODES])
        pT = sb("pT", [128, 2, HEADS, NODES])
        rsum = sb("rsum", [128, 2, HEADS])
        attn = sb("attn", [128, 2, D])
        attnT = sb("attnT", [128, 2, KT, NODES])
        x1 = sb("x1", [128, PER, D])
        n2 = sb("n2", [128, PER, D])
        x1_b2 = sb("x1_b2", [128, PER, D])
        n2T = sb("n2T", [128, KT, TOK])
        hT = sb("hT", [128, HT, TOK])
        x2 = sb("x2", [128, PER, D])
        x2_bo = sb("x2_bo", [128, PER, D])
        x2T = sb("x2T", [128, KT, TOK])
        tT = sb("tT", [128, KT, TOK])
        vo = sb("vo", [128, PER, D])
        neg_s1 = sb("neg_s1", [128, PER, NODES])
        neg_max1 = sb("neg_max1", [128, PER])
        p1 = sb("p1", [128, PER, NODES])
        sum1 = sb("sum1", [128, PER])
        rsum1 = sb("rsum1", [128, PER])
        p1T = sb("p1T", [128, PER, NODES])
        y = sb("y", [128, PER, D])
        n3 = sb("n3", [128, PER, D])
        n3g = sb("n3g", [128, PER, D])
        outs = sb("outs", [128, PER, D])
        lns = {n: dict(stats=sb(f"stats{n}", [128, PER, 6]), mv=sb(f"mv{n}", [128, PER, 2]),
                       ve=sb(f"ve{n}", [128, PER]), rstd=sb(f"rstd{n}", [128, PER]),
                       shift=sb(f"shift{n}", [128, PER])) for n in (1, 2, 3)}

        bank = [ctx.enter_context(nc.psum_tensor(f"bank{i}", [128, 512], f32)) for i in range(8)]

        w_load = sem("w_load")
        x_load = sem("x_load")
        adj_load = sem("adj_load")
        out_store = sem("out_store")
        consts = sem("consts")
        prep_pe = sem("prep_pe")
        prep_dve = sem("prep_dve")
        stand_dve, stand_pool = sem("stand_dve"), sem("stand_pool")
        pe_nxT = sem("pe_nxT")
        pe_k, pe_q, pe_v = sem("pe_k"), sem("pe_q"), sem("pe_v")
        pe_s, pe_pT, pe_av = sem("pe_s"), sem("pe_pT"), sem("pe_av")
        pe_attnT, pe_wo = sem("pe_attnT"), sem("pe_wo")
        pe_n2T = sem("pe_n2T")
        pe_up = sem("pe_up")
        pe_down = sem("pe_down")
        pe_x2T = sem("pe_x2T")
        pe_t, pe_vo = sem("pe_t"), sem("pe_vo")
        pe_s1, pe_p1T = sem("pe_s1"), sem("pe_p1T")
        pe_av1 = sem("pe_av1")
        act_nxT, act_k = sem("act_nxT"), sem("act_k")
        act_q = sem("act_q")
        act_p = sem("act_p")
        act_pT, act_attnT = sem("act_pT"), sem("act_attnT")
        act_n2T = sem("act_n2T")
        act_h = sem("act_h")
        act_x2T, act_t, act_vo = sem("act_x2T"), sem("act_t"), sem("act_vo")
        act_p1 = sem("act_p1")
        ln_dve = {n: sem(f"ln{n}_dve") for n in (1, 2, 3)}
        dve_nxT, dve_k = sem("dve_nxT"), sem("dve_k")
        dve_v = sem("dve_v")
        dve_s = sem("dve_s")
        dve_pT, dve_r, dve_attn = sem("dve_pT"), sem("dve_r"), sem("dve_attn")
        dve_x1 = sem("dve_x1")
        dve_n2T = sem("dve_n2T")
        dve_x2 = sem("dve_x2")
        dve_x2T, dve_t, dve_vo = sem("dve_x2T"), sem("dve_t"), sem("dve_vo")
        dve_s1 = sem("dve_s1")
        dve_p1T, dve_r1 = sem("dve_p1T"), sem("dve_r1")
        dve_y = sem("dve_y")
        ln_pool = {n: sem(f"ln{n}_pool") for n in (1, 2, 3)}
        pool_adj = sem("pool_adj")
        pool_bias = sem("pool_bias")
        pool_pen1 = sem("pool_pen1")
        pool_xbo, pool_x1b, pool_x2b = sem("pool_xbo"), sem("pool_x1b"), sem("pool_x2b")
        pool_out = sem("pool_out")

        weight_loads = [(wq_s, wq), (wk_s, wk), (wv_s, wv), (wo_s, wo), (w1_s, w1), (w2_s, w2),
                        (l1_raw["wq1"], wq1), (l1_raw["wk1"], wk1), (l1_raw["wv1"], wv1), (wo1_s, wo1)]
        col_loads = [(cols["ln1_g"], ln1_g), (cols["ln1_b"], ln1_b), (cols["ln2_g"], ln2_g),
                     (cols["ln2_b"], ln2_b), (cols["bq"], bq), (cols["bk"], bk), (b1_c, b1)]
        row_loads = [(rows["bv"], bv), (rows["bo"], bo), (rows["b2"], b2), (rows["bo1"], bo1),
                     (rows["gamma"], gamma), (rows["beta"], beta)]
        W_ALL = 16 * (len(weight_loads) + len(col_loads) + len(row_loads))

        block = ctx.enter_context(nc.Block())

        @block.sync
        def _(sp):
            def load(g):
                sp.wait_ge(ln_dve[1], LN_STEPS * g)
                sp.wait_ge(pool_xbo, g)
                sp.dma_start(xs[:, :, :], x_v[g]).then_inc(x_load, 16)
                sp.wait_ge(pool_adj, g)
                sp.dma_start(adj_i[:, :, :], adj_v[g]).then_inc(adj_load, 16)

            def store(g):
                sp.wait_ge(pool_out, 2 * g + 2)
                sp.dma_start(out_v[g], outs[:, :, :]).then_inc(out_store, 16)

            load(0)
            for dst, src in weight_loads:
                sp.dma_start(dst[:, :, :], src.rearrange("(t p) n -> p t n", p=128)).then_inc(w_load, 16)
            for g in range(1, 4):
                load(g)
            store(0)
            with sp.Fori(1, GROUPS - 3) as g:
                load(g + 3)
                store(g)
            for g in range(GROUPS - 3, GROUPS):
                store(g)
            sp.wait_ge(out_store, 16 * GROUPS)

        @block.tensor
        def _(pe):
            mm, tr = nc.tensor.matmul, nc.tensor.transpose

            pe.wait_ge(w_load, W_ALL)
            pe.wait_ge(consts, CONSTS)
            for i, n in enumerate(("wq1", "wk1", "wv1")):
                for c in range(KT):
                    for r in range(KT):
                        last = tr(bank[2 * i + c][:, 128 * r:128 * r + 128],
                                  l1_raw[n][:, r, 128 * c:128 * c + 128], ident[:, :])
                last.then_inc(prep_pe, 1)
            pe.wait_ge(prep_dve, 3)
            for m in range(KT):
                for c in range(KT):
                    last = mm(bank[6][:, 256 * m:256 * m + 256], l1_T["wq1"][:, c, 128 * m:128 * m + 128],
                              l1_T["wk1"][:, c, :], start=(c == 0), stop=(c == KT - 1))
            last.then_inc(prep_pe, 1)
            for m in range(KT):
                for c in range(KT):
                    last = mm(bank[7][:, 256 * m:256 * m + 256], l1_T["wv1"][:, c, 128 * m:128 * m + 128],
                              wo1_s[:, c, :], start=(c == 0), stop=(c == KT - 1))
            last.then_inc(prep_pe, 1)
            pe.wait_ge(prep_dve, 5)

            def nodes(b):
                return slice(128 * b, 128 * b + 128)

            def norm_transpose(g):
                pe.wait_ge(ln_dve[1], LN_STEPS * g + LN_STEPS)
                pe.wait_ge(act_pT, 4 * g)
                pe.wait_ge(dve_pT, 4 * g)
                for t in range(KT):
                    for b in range(PER):
                        last = tr(bank[2 + t][:, nodes(b)], nx[:, b, 128 * t:128 * t + 128], ident[:, :])
                last.then_inc(pe_nxT, 1)

            def project_k(g):
                pe.wait_ge(act_nxT, g + 1)
                pe.wait_ge(dve_nxT, g + 1)
                for m in range(KT):
                    for t in range(KT):
                        last = mm(bank[2 + m][:, :], wk_s[:, t, 128 * m:128 * m + 128], nxT[:, t, :],
                                  start=(t == 0), stop=(t == KT - 1))
                    last.then_inc(pe_k, 1)

            def project_q(g):
                pe.wait_ge(dve_s, 4 * g)
                for m in range(KT):
                    for t in range(KT):
                        last = mm(bank[m][:, :], wq_s[:, t, 128 * m:128 * m + 128], nxT[:, t, :],
                                  start=(t == 0), stop=(t == KT - 1))
                    last.then_inc(pe_q, 1)

            def project_v(g):
                pe.wait_ge(dve_attn, 4 * g)
                pe.wait_ge(dve_x1, 4 * g)
                for half in range(2):
                    for b in (2 * half, 2 * half + 1):
                        for t in range(KT):
                            last = mm(bank[4 + half][:, 256 * (b % 2):256 * (b % 2) + 256],
                                      nxT[:, t, nodes(b)], wv_s[:, t, :], start=(t == 0), stop=(t == KT - 1))
                    last.then_inc(pe_v, 1)

            def scores(g, b):
                if b == 0:
                    pe.wait_ge(act_q, 2 * g + 2)
                    pe.wait_ge(act_k, 4 * g + 4)
                    pe.wait_ge(dve_k, 4 * g + 4)
                else:
                    pe.wait_ge(dve_s, 4 * g + b)
                for t in range(KT):
                    last = mm(bank[t][:, :], qT[:, t, nodes(b)], k_diag[:, t, :, nodes(b)], start=True, stop=True)
                last.then_inc(pe_s, 1)

            def p_transpose(g, b):
                pe.wait_ge(act_p, 4 * g + b + 1)
                if b > 0:
                    pe.wait_ge(act_pT, 4 * g + b)
                    pe.wait_ge(dve_pT, 4 * g + b)
                for h in range(HEADS):
                    last = tr(bank[2 + h // HPT][:, nodes(h % HPT)], p_s[:, b % 2, h, :], ident[:, :])
                last.then_inc(pe_pT, 1)

            def attend(g, b):
                pe.wait_ge(act_pT, 4 * g + b + 1)
                pe.wait_ge(dve_pT, 4 * g + b + 1)
                pe.wait_ge(dve_v, 2 * g + 2)
                pe.wait_ge(dve_attn, 4 * g + b)
                for h in range(HEADS):
                    last = mm(bank[4][:, (HD + 1) * h:(HD + 1) * (h + 1)], pT[:, b % 2, h, :],
                              v_one[:, b, h, :], start=True, stop=True)
                last.then_inc(pe_av, 1)

            def attn_transpose(g, b):
                pe.wait_ge(dve_attn, 4 * g + b + 1)
                pe.wait_ge(dve_x1, 4 * g + b)
                for t in range(KT):
                    last = tr(bank[5][:, nodes(t)], attn[:, b % 2, 128 * t:128 * t + 128], ident[:, :])
                last.then_inc(pe_attnT, 1)

            def out_project(g, b):
                pe.wait_ge(act_attnT, 4 * g + b + 1)
                for t in range(KT):
                    last = mm(bank[5][:, 0:D], attnT[:, b % 2, t, :], wo_s[:, t, :], start=(t == 0), stop=(t == KT - 1))
                last.then_inc(pe_wo, 1)

            def n2_transpose(g):
                pe.wait_ge(ln_dve[2], LN_STEPS * g + LN_STEPS)
                pe.wait_ge(dve_y, 4 * g)
                for t in range(KT):
                    for b in range(PER):
                        last = tr(bank[6 + t][:, nodes(b)], n2[:, b, 128 * t:128 * t + 128], ident[:, :])
                last.then_inc(pe_n2T, 1)

            def mlp_up(g, j):
                if j == 0:
                    pe.wait_ge(act_n2T, g + 1)
                    pe.wait_ge(dve_n2T, g + 1)
                elif j >= 2:
                    pe.wait_ge(act_h, HT * g + j - 1)
                for t in range(KT):
                    last = mm(bank[6 + j % 2][:, :], w1_s[:, t, 128 * j:128 * j + 128], n2T[:, t, :],
                              start=(t == 0), stop=(t == KT - 1))
                last.then_inc(pe_up, 1)

            def mlp_down(g, b):
                pe.wait_ge(act_h, HT * g + HT)
                if b >= 2:
                    pe.wait_ge(dve_x2, 4 * g + b - 1)
                for j in range(HT):
                    last = mm(bank[6 + b % 2][:, 0:D], hT[:, j, nodes(b)], w2_s[:, j, :],
                              start=(j == 0), stop=(j == HT - 1))
                last.then_inc(pe_down, 1)

            def x2_transpose(g):
                pe.wait_ge(dve_x2, 4 * g + 4)
                for t in range(KT):
                    for b in range(PER):
                        last = tr(bank[6 + t][:, nodes(b)], x2[:, b, 128 * t:128 * t + 128], ident[:, :])
                last.then_inc(pe_x2T, 1)

            def t_project(g):
                pe.wait_ge(act_x2T, g + 1)
                pe.wait_ge(dve_x2T, g + 1)
                for m in range(KT):
                    for t in range(KT):
                        last = mm(bank[6 + m][:, :], qk1[:, t, 128 * m:128 * m + 128], x2T[:, t, :],
                                  start=(t == 0), stop=(t == KT - 1))
                    last.then_inc(pe_t, 1)

            def scores1(g):
                pe.wait_ge(act_t, g + 1)
                pe.wait_ge(dve_t, g + 1)
                for b in range(PER):
                    for t in range(KT):
                        last = mm(bank[6][:, nodes(b)], tT[:, t, nodes(b)], x2T[:, t, nodes(b)],
                                  start=(t == 0), stop=(t == KT - 1))
                last.then_inc(pe_s1, 1)

            def vo_project(g, half):
                if half == 1:
                    pe.wait_ge(dve_s1, g + 1)
                for b in (2 * half, 2 * half + 1):
                    for t in range(KT):
                        last = mm(bank[7 - half][:, 256 * (b % 2):256 * (b % 2) + 256], x2T[:, t, nodes(b)],
                                  vo1[:, t, :], start=(t == 0), stop=(t == KT - 1))
                last.then_inc(pe_vo, 1)

            def p1_transpose(g):
                pe.wait_ge(act_p1, 4 * g + 4)
                pe.wait_ge(act_vo, g + 1)
                for b in range(PER):
                    last = tr(bank[7][:, nodes(b)], p1[:, b, :], ident[:, :])
                last.then_inc(pe_p1T, 1)

            def attend1(g):
                pe.wait_ge(dve_p1T, g + 1)
                pe.wait_ge(dve_vo, g + 1)
                for half in range(2):
                    for b in (2 * half, 2 * half + 1):
                        last = mm(bank[6 + half][:, 256 * (b % 2):256 * (b % 2) + 256], p1T[:, b, :], vo[:, b, :],
                                  start=True, stop=True)
                    last.then_inc(pe_av1, 1)

            def turn(gp, ga, gb):
                P, A, B = gp is not None, ga is not None, gb is not None
                if B:
                    for j in range(HT):
                        mlp_up(gb, j)
                for k in range(PER + 1):
                    if A and k < PER:
                        scores(ga, k)
                    if A and k >= 1:
                        p_transpose(ga, k - 1)
                    if A and k >= 2:
                        attn_transpose(ga, k - 2)
                    if B and k < PER:
                        mlp_down(gb, k)
                    if B and k == PER:
                        x2_transpose(gb)
                    if A and k >= 1:
                        attend(ga, k - 1)
                    if A and k >= 2:
                        out_project(ga, k - 2)
                if B:
                    t_project(gb)
                if A:
                    attn_transpose(ga, PER - 1)
                if P:
                    norm_transpose(gp)
                if B:
                    scores1(gb)
                if A:
                    out_project(ga, PER - 1)
                if B:
                    vo_project(gb, 0)
                    vo_project(gb, 1)
                    p1_transpose(gb)
                if P:
                    project_k(gp)
                if B:
                    attend1(gb)
                if P:
                    project_q(gp)
                if A:
                    n2_transpose(ga)
                if P:
                    project_v(gp)

            turn(0, None, None)
            turn(1, 0, None)
            turn(2, 1, 0)
            with pe.Fori(2, GROUPS - 1) as g:
                turn(g + 1, g, g - 1)
            turn(None, GROUPS - 1, GROUPS - 2)
            turn(None, None, GROUPS - 1)

        @block.scalar
        def _(act):
            run = nc.scalar.activation
            for dst, src in col_loads:
                with nc.allow_non_contiguous_dma(reason="a bias vector onto partitions"):
                    act.dma_start(dst[:, :], src.rearrange("(t p) -> p t", p=128)).then_inc(w_load, 16)
            for dst, src in row_loads:
                act.dma_start(dst[:, :], src.rearrange("(a d) -> a d", a=1).to_broadcast([128, D])).then_inc(w_load, 16)
            act.wait_ge(w_load, W_ALL)
            act.wait_ge(prep_dve, 6)
            act.wait_ge(consts, CONSTS)

            def nxT_copy(g):
                act.wait_ge(pe_nxT, g + 1)
                act.wait_ge(pe_v, 2 * g)
                run(nxT[:, 0, :], bank[2][:, :], ACT.Identity, scale=cols["ln1_g"][:, 0:1],
                    bias=cols["ln1_b"][:, 0:1]).then_inc(act_nxT, 1)

            def k_copy(g):
                act.wait_ge(pe_k, 2 * g + 1)
                act.wait_ge(pe_s, 4 * g)
                for r in range(HPT):
                    s = slice(HD * r, HD * r + HD)
                    run(k_diag[s, 0, r, :], bank[2][s, :], ACT.Identity, bias=cols["bk"][s, 0:1]).then_inc(act_k, 1)

            def q_copy(g):
                for t in range(KT):
                    act.wait_ge(pe_q, 2 * g + t + 1)
                    run(qT[:, t, :], bank[t][:, :], ACT.Identity, scale=SCALE0, bias=bqs[:, t:t + 1]).then_inc(act_q, 1)

            def exps(g, b):
                act.wait_ge(dve_s, 4 * g + b + 1)
                act.wait_ge(pe_pT, 4 * g + max(b - 1, 0))
                for h in range(HEADS):
                    last = run(p_s[:, b % 2, h, :], neg_s[:, b % 2, h, :], ACT.Exp, scale=-1.0,
                               bias=neg_max[:, b % 2, h:h + 1])
                last.then_inc(act_p, 1)

            def pT_copy(g, b):
                act.wait_ge(pe_pT, 4 * g + b + 1)
                act.wait_ge(pe_av, 4 * g + max(b - 1, 0))
                run(pT[:, b % 2, 0:HPT, :], bank[2][:, :].rearrange("p (h n) -> p h n", h=HPT),
                    ACT.Identity).then_inc(act_pT, 1)

            def attnT_copy(g, b):
                act.wait_ge(pe_attnT, 4 * g + b + 1)
                act.wait_ge(pe_wo, 4 * g + max(b - 1, 0))
                run(attnT[:, b % 2, :, :], bank[5][:, 0:D].rearrange("p (t n) -> p t n", t=KT),
                    ACT.Identity).then_inc(act_attnT, 1)

            def n2T_copy(g):
                act.wait_ge(pe_n2T, g + 1)
                act.wait_ge(pe_up, HT * g)
                run(n2T[:, 0, :], bank[6][:, :], ACT.Identity, scale=cols["ln2_g"][:, 0:1],
                    bias=cols["ln2_b"][:, 0:1]).then_inc(act_n2T, 1)

            def gelu(g, j):
                act.wait_ge(pe_up, HT * g + j + 1)
                if j == 0:
                    act.wait_ge(pe_down, 4 * g)
                run(hT[:, j, :], bank[6 + j % 2][:, :], ACT.Gelu, bias=b1_c[:, j:j + 1]).then_inc(act_h, 1)

            def x2T_copy(g):
                act.wait_ge(pe_x2T, g + 1)
                act.wait_ge(pe_vo, 2 * g)
                run(x2T[:, 0, :], bank[6][:, :], ACT.Identity).then_inc(act_x2T, 1)

            def t_copy(g):
                act.wait_ge(pe_t, 2 * g + 1)
                act.wait_ge(pe_s1, g)
                run(tT[:, 0, :], bank[6][:, :], ACT.Identity).then_inc(act_t, 1)

            def exps1(g):
                act.wait_ge(dve_s1, g + 1)
                act.wait_ge(pe_p1T, g)
                act.wait_ge(dve_r1, g)
                for b in range(PER):
                    run(p1[:, b, :], neg_s1[:, b, :], ACT.Exp, scale=-1.0, bias=neg_max1[:, b:b + 1],
                        accum_out=sum1[:, b:b + 1]).then_inc(act_p1, 1)

            def vo_copy(g):
                act.wait_ge(pe_vo, 2 * g + 1)
                act.wait_ge(pe_av1, 2 * g)
                run(vo[:, 0:2, :], bank[7][:, :].rearrange("p (b d) -> p b d", b=2), ACT.Identity).then_inc(act_vo, 1)

            def turn(gp, ga, gb):
                P, A, B = gp is not None, ga is not None, gb is not None
                if B:
                    for j in range(HT):
                        gelu(gb, j)
                for k in range(PER + 1):
                    if A and k >= 1:
                        pT_copy(ga, k - 1)
                    if A and k >= 2:
                        attnT_copy(ga, k - 2)
                    if A and k < PER:
                        exps(ga, k)
                if B:
                    x2T_copy(gb)
                    t_copy(gb)
                if A:
                    attnT_copy(ga, PER - 1)
                if P:
                    nxT_copy(gp)
                if B:
                    exps1(gb)
                    vo_copy(gb)
                if P:
                    k_copy(gp)
                    q_copy(gp)
                if A:
                    n2T_copy(ga)
                    run(gelu_probe[:, :], minus_half[:, 0:1], ACT.Gelu)

            turn(0, None, None)
            turn(1, 0, None)
            turn(2, 1, 0)
            with act.Fori(2, GROUPS - 1) as g:
                turn(g + 1, g, g - 1)
            turn(None, GROUPS - 1, GROUPS - 2)
            turn(None, None, GROUPS - 1)

        @block.vector
        def _(dve):
            V = nc.vector
            V.memset(v_one[:, :, :, :], 1.0).then_inc(consts, 1)
            V.memset(minus_half[:, :], -0.5).then_inc(consts, 1)
            for i, n in enumerate(("wq1", "wk1", "wv1")):
                dve.wait_ge(prep_pe, i + 1)
                for c in range(KT):
                    last = V.tensor_copy(l1_T[n][:, c, :], bank[2 * i + c][:, 0:D])
                last.then_inc(prep_dve, 1)
            dve.wait_ge(prep_pe, 4)
            V.tensor_scalar(qk1[:, :, :], bank[6][:, :].rearrange("p (m d) -> p m d", m=KT), SCALE1, None,
                            ALU.mult).then_inc(prep_dve, 1)
            dve.wait_ge(prep_pe, 5)
            V.tensor_copy(vo1[:, :, :], bank[7][:, :].rearrange("p (m d) -> p m d", m=KT)).then_inc(prep_dve, 1)
            dve.wait_ge(w_load, W_ALL)
            V.tensor_scalar(bqs[:, :], cols["bq"][:, :], SCALE0, None, ALU.mult).then_inc(prep_dve, 1)
            dve.wait_ge(consts, CONSTS)

            def moments(n, g, src):
                t, s, base = lns[n], ln_dve[n], LN_STEPS * g
                for b in range(PER):
                    V.bn_stats(t["stats"][:, b, :], src[:, b, :]).then_inc(s, 1)
                dve.wait_ge(s, base + 4)
                dve.sem_inc(stand_dve, 1)
                for b in range(PER):
                    V.bn_aggr(t["mv"][:, b, :], t["stats"][:, b, :]).then_inc(s, 1)
                dve.wait_ge(s, base + 8)
                dve.wait_ge(ln_pool[n], g)
                V.tensor_scalar(t["ve"][:, :], t["mv"][:, :, 1], EPS, None, ALU.add).then_inc(s, 1)

            def normed(n, g, src, dst):
                t, s, base = lns[n], ln_dve[n], LN_STEPS * g
                dve.wait_ge(ln_pool[n], g + 1)
                V.scalar_tensor_tensor(out=t["shift"][:, :], in0=t["mv"][:, :, 0], scalar=-1.0, in1=t["rstd"][:, :],
                                       op0=ALU.mult, op1=ALU.mult).then_inc(s, 1)
                dve.wait_ge(s, base + 10)
                for b in range(PER):
                    V.tensor_scalar(dst[:, b, :], src[:, b, :], t["rstd"][:, b:b + 1], t["shift"][:, b:b + 1],
                                    ALU.mult, ALU.add).then_inc(s, 1)

            def norm1(g):
                dve.wait_ge(x_load, 16 * g + 16)
                moments(1, g, xs)
                dve.wait_ge(pe_nxT, g)
                normed(1, g, xs, nx)

            def nxT_copy(g):
                dve.wait_ge(pe_nxT, g + 1)
                dve.wait_ge(pe_v, 2 * g)
                V.tensor_scalar(nxT[:, 1, :], bank[3][:, :], cols["ln1_g"][:, 1:2], cols["ln1_b"][:, 1:2],
                                ALU.mult, ALU.add).then_inc(dve_nxT, 1)

            def k_copy(g):
                dve.wait_ge(pe_k, 2 * g + 2)
                dve.wait_ge(pe_s, 4 * g)
                for r in range(HPT):
                    s = slice(HD * r, HD * r + HD)
                    V.tensor_scalar(k_diag[s, 1, r, :], bank[3][s, :], cols["bk"][s, 1:2], None,
                                    ALU.add).then_inc(dve_k, 1)

            def v_copy(g):
                dve.wait_ge(pe_av, 4 * g)
                for half in range(2):
                    dve.wait_ge(pe_v, 2 * g + half + 1)
                    for i in range(2):
                        last = V.tensor_tensor(v_one[:, 2 * half + i, :, 0:HD],
                                               bank[4 + half][:, D * i:D * i + D].rearrange("p (h d) -> p h d", h=HEADS),
                                               rows["bv"][:, :].rearrange("p (h d) -> p h d", h=HEADS), ALU.add)
                    last.then_inc(dve_v, 1)

            def biased(g, b):
                dve.wait_ge(pe_s, 4 * g + b + 1)
                if b == 0:
                    dve.wait_ge(pool_bias, 4 * g + 4)
                dve.wait_ge(act_p, 4 * g + max(b - 1, 0))
                dve.sem_inc(stand_dve, 1)
                for h in range(HEADS):
                    last = V.tensor_tensor_reduce(neg_s[:, b % 2, h, :], bank[h // HPT][:, NODES * (h % HPT):NODES * (h % HPT) + NODES],
                                                  bias0[:, b, :], -1.0, -3.0 * MASKED, ALU.add, ALU.min,
                                                  neg_max[:, b % 2, h:h + 1])
                last.then_inc(dve_s, 1)

            def pT_copy(g, b):
                dve.wait_ge(pe_pT, 4 * g + b + 1)
                dve.wait_ge(pe_av, 4 * g + max(b - 1, 0))
                V.tensor_copy(pT[:, b % 2, HPT:HEADS, :],
                              bank[3][:, :].rearrange("p (h n) -> p h n", h=HPT)).then_inc(dve_pT, 1)

            def normalise(g, b):
                dve.wait_ge(pe_av, 4 * g + b + 1)
                dve.wait_ge(pe_attnT, 4 * g + max(b - 1, 0))
                av = bank[4][:, 0:HEADS * (HD + 1)].rearrange("p (h d) -> p h d", h=HEADS)
                V.reciprocal(rsum[:, b % 2, :], av[:, :, HD]).then_inc(dve_r, 1)
                dve.wait_ge(dve_r, 4 * g + b + 1)
                V.tensor_tensor(attn[:, b % 2, :].rearrange("p (h d) -> p h d", h=HEADS), av[:, :, 0:HD],
                                rsum[:, b % 2, :, None].to_broadcast([128, HEADS, HD]), ALU.mult).then_inc(dve_attn, 1)

            def residual1(g, b):
                dve.wait_ge(pe_wo, 4 * g + b + 1)
                if b == 0:
                    dve.wait_ge(pool_xbo, g + 1)
                    dve.wait_ge(pool_x1b, g)
                V.tensor_tensor(x1[:, b, :], bank[5][:, 0:D], x_bo[:, b, :], ALU.add).then_inc(dve_x1, 1)

            def moments2(g):
                dve.wait_ge(dve_x1, 4 * g + 4)
                moments(2, g, x1)

            def norm2(g):
                dve.wait_ge(pe_n2T, g)
                normed(2, g, x1, n2)

            def n2T_copy(g):
                dve.wait_ge(pe_n2T, g + 1)
                dve.wait_ge(pe_up, HT * g)
                V.tensor_scalar(n2T[:, 1, :], bank[7][:, :], cols["ln2_g"][:, 1:2], cols["ln2_b"][:, 1:2],
                                ALU.mult, ALU.add).then_inc(dve_n2T, 1)

            def residual2(g, b):
                dve.wait_ge(pe_down, 4 * g + b + 1)
                if b == 0:
                    dve.wait_ge(pool_x1b, g + 1)
                    dve.wait_ge(pool_x2b, g)
                    dve.wait_ge(pe_x2T, g)
                V.tensor_tensor(x2[:, b, :], bank[6 + b % 2][:, 0:D], x1_b2[:, b, :], ALU.add).then_inc(dve_x2, 1)

            def x2T_copy(g):
                dve.wait_ge(pe_x2T, g + 1)
                dve.wait_ge(pe_vo, 2 * g)
                V.tensor_copy(x2T[:, 1, :], bank[7][:, :]).then_inc(dve_x2T, 1)

            def t_copy(g):
                dve.wait_ge(pe_t, 2 * g + 2)
                dve.wait_ge(pe_s1, g)
                V.tensor_copy(tT[:, 1, :], bank[7][:, :]).then_inc(dve_t, 1)

            def biased1(g):
                dve.wait_ge(pe_s1, g + 1)
                dve.wait_ge(pool_pen1, g + 1)
                dve.wait_ge(act_p1, 4 * g)
                dve.sem_inc(stand_dve, 1)
                for b in range(PER):
                    last = V.tensor_tensor_reduce(neg_s1[:, b, :], bank[6][:, NODES * b:NODES * b + NODES],
                                                  pen1[:, b, :], -1.0, -3.0 * MASKED, ALU.add, ALU.min, neg_max1[:, b:b + 1])
                last.then_inc(dve_s1, 1)

            def vo_copy(g):
                dve.wait_ge(pe_vo, 2 * g + 2)
                dve.wait_ge(pe_av1, 2 * g)
                V.tensor_copy(vo[:, 2:4, :], bank[6][:, :].rearrange("p (b d) -> p b d", b=2)).then_inc(dve_vo, 1)

            def p1T_copy(g):
                dve.wait_ge(pe_p1T, g + 1)
                dve.wait_ge(pe_av1, 2 * g)
                V.tensor_copy(p1T[:, :, :], bank[7][:, :].rearrange("p (b n) -> p b n", b=PER)).then_inc(dve_p1T, 1)
                dve.wait_ge(act_p1, 4 * g + 4)
                V.reciprocal(rsum1[:, :], sum1[:, :]).then_inc(dve_r1, 1)

            def residual3(g):
                dve.wait_ge(dve_r1, g + 1)
                dve.wait_ge(pool_x2b, g + 1)
                for b in range(PER):
                    if b % 2 == 0:
                        dve.wait_ge(pe_av1, 2 * g + b // 2 + 1)
                    V.scalar_tensor_tensor(out=y[:, b, :], in0=bank[6 + b // 2][:, D * (b % 2):D * (b % 2) + D],
                                           scalar=rsum1[:, b:b + 1], in1=x2_bo[:, b, :],
                                           op0=ALU.mult, op1=ALU.add).then_inc(dve_y, 1)

            def moments3(g):
                dve.wait_ge(dve_y, 4 * g + 4)
                moments(3, g, y)

            def norm3(g):
                dve.wait_ge(pool_out, 2 * g)
                normed(3, g, y, n3)

            def turn(gp, ga, gb):
                P, A, B = gp is not None, ga is not None, gb is not None
                if P:
                    norm1(gp)
                for k in range(PER + 1):
                    if A and k < PER:
                        biased(ga, k)
                    if A and k >= 1:
                        pT_copy(ga, k - 1)
                    if B and k < PER:
                        residual2(gb, k)
                    if B and k == PER:
                        x2T_copy(gb)
                    if A and k >= 1:
                        normalise(ga, k - 1)
                    if A and k >= 2:
                        residual1(ga, k - 2)
                if B:
                    t_copy(gb)
                if P:
                    nxT_copy(gp)
                if B:
                    biased1(gb)
                if A:
                    residual1(ga, PER - 1)
                    moments2(ga)
                if B:
                    vo_copy(gb)
                    p1T_copy(gb)
                if A:
                    norm2(ga)
                if P:
                    k_copy(gp)
                if B:
                    residual3(gb)
                    moments3(gb)
                if A:
                    n2T_copy(ga)
                if P:
                    v_copy(gp)
                if B:
                    norm3(gb)

            turn(0, None, None)
            turn(1, 0, None)
            turn(2, 1, 0)
            with dve.Fori(2, GROUPS - 1) as g:
                turn(g + 1, g, g - 1)
            turn(None, GROUPS - 1, GROUPS - 2)
            turn(None, None, GROUPS - 1)

        @block.gpsimd
        def _(pool):
            P = nc.gpsimd
            P.memset(k_diag[:, :, :, :], 0.0).then_inc(consts, 1)
            P.memset(ident[:, :], 0.0).then_inc(consts, 1)
            pool.wait_ge(consts, 4)
            P.affine_select(out=ident[:, :], in_=ident[:, :], compare_op=ALU.not_equal, fill=1.0, base=0,
                            pattern=[[-1, 128]], channel_multiplier=1).then_inc(consts, 1)
            pool.wait_ge(w_load, W_ALL)

            def rstd(n, g):
                pool.wait_ge(ln_dve[n], LN_STEPS * g + 9)
                P.tensor_tensor(lns[n]["rstd"][:, :], lns[n]["ve"][:, :], minus_half[:, :], ALU.pow).then_inc(ln_pool[n], 1)

            def bias(g):
                pool.wait_ge(adj_load, 16 * g + 16)
                pool.wait_ge(pool_pen1, g)
                pool.sem_inc(stand_pool, 1)
                P.tensor_copy(adj_f[:, :, :], adj_i[:, :, :]).then_inc(pool_adj, 1)
                pool.wait_ge(pool_adj, g + 1)
                pool.sem_inc(stand_pool, 1)
                P.tensor_scalar(tenth[:, :, :], adj_f[:, :, :], 0.1, None, ALU.mult).then_inc(pool_bias, 1)
                P.tensor_scalar(pen0[:, :, :], adj_f[:, :, :], 0.0, MASKED, ALU.is_le, ALU.mult).then_inc(pool_bias, 1)
                pool.wait_ge(dve_s, 4 * g)
                pool.wait_ge(pool_bias, 4 * g + 2)
                P.tensor_tensor(bias0[:, :, :], tenth[:, :, :], adj_f[:, :, :], ALU.mult).then_inc(pool_bias, 1)
                pool.wait_ge(pool_bias, 4 * g + 3)
                P.tensor_tensor(bias0[:, :, :], bias0[:, :, :], pen0[:, :, :], ALU.add).then_inc(pool_bias, 1)

            def x_plus_bo(g):
                pool.wait_ge(x_load, 16 * g + 16)
                pool.wait_ge(dve_x1, 4 * g)
                P.tensor_tensor(x_bo[:, :, :], xs[:, :, :],
                                rows["bo"][:, None, :].to_broadcast([128, PER, D]), ALU.add).then_inc(pool_xbo, 1)

            def mask1(g):
                pool.wait_ge(dve_s1, g)
                pool.sem_inc(stand_pool, 1)
                P.tensor_scalar(pen1[:, :, :], adj_f[:, :, :], 0.0, MASKED, ALU.is_equal, ALU.mult).then_inc(pool_pen1, 1)

            def x1_plus_b2(g):
                pool.wait_ge(dve_x1, 4 * g + 4)
                pool.wait_ge(dve_x2, 4 * g)
                P.tensor_tensor(x1_b2[:, :, :], x1[:, :, :],
                                rows["b2"][:, None, :].to_broadcast([128, PER, D]), ALU.add).then_inc(pool_x1b, 1)

            def x2_plus_bo(g):
                pool.wait_ge(dve_x2, 4 * g + 4)
                pool.wait_ge(dve_y, 4 * g)
                P.tensor_tensor(x2_bo[:, :, :], x2[:, :, :],
                                rows["bo1"][:, None, :].to_broadcast([128, PER, D]), ALU.add).then_inc(pool_x2b, 1)

            def finish(g):
                pool.wait_ge(ln_dve[3], LN_STEPS * g + LN_STEPS)
                P.tensor_tensor(n3g[:, :, :], n3[:, :, :],
                                rows["gamma"][:, None, :].to_broadcast([128, PER, D]), ALU.mult).then_inc(pool_out, 1)
                pool.wait_ge(pool_out, 2 * g + 1)
                pool.wait_ge(out_store, 16 * g)
                P.tensor_tensor(outs[:, :, :], n3g[:, :, :],
                                rows["beta"][:, None, :].to_broadcast([128, PER, D]), ALU.add).then_inc(pool_out, 1)

            def turn(gp, ga, gb):
                P, A, B = gp is not None, ga is not None, gb is not None
                if P:
                    rstd(1, gp)
                if B:
                    x2_plus_bo(gb)
                if A:
                    mask1(ga)
                    rstd(2, ga)
                    x1_plus_b2(ga)
                if P:
                    x_plus_bo(gp)
                if B:
                    rstd(3, gb)
                if P:
                    bias(gp)
                if B:
                    finish(gb)

            turn(0, None, None)
            turn(1, 0, None)
            turn(2, 1, 0)
            with pool.Fori(2, GROUPS - 1) as g:
                turn(g + 1, g, g - 1)
            turn(None, GROUPS - 1, GROUPS - 2)
            turn(None, None, GROUPS - 1)


_INS = ['x', 'adj', 'L0_gnn_ln1_g', 'L0_gnn_ln1_b', 'L0_gnn_ln2_g', 'L0_gnn_ln2_b', 'L0_gnn_wq', 'L0_gnn_bq',
        'L0_gnn_wk', 'L0_gnn_bk', 'L0_gnn_wv', 'L0_gnn_bv', 'L0_gnn_wo', 'L0_gnn_bo', 'L0_gnn_w1', 'L0_gnn_b1',
        'L0_gnn_w2', 'L0_gnn_b2', 'L1_gnn_Wq', 'L1_gnn_Wk', 'L1_gnn_Wv', 'L1_gnn_Wo', 'L1_gnn_bo',
        'L1_gnn_gamma', 'L1_gnn_beta']


def kernel(**inputs):
    import numpy as _np
    import concourse.bacc as _bacc
    from concourse import mybir as _mybir
    from concourse.bass_utils import run_bass_kernel_spmd as _run

    nc = _bacc.Bacc("TRN2", target_bir_lowering=False, num_devices=1)
    arrays, args = {}, []
    for name in _INS:
        a = _np.ascontiguousarray(inputs[name])
        arrays[f"in_{name}"] = a
        args.append(nc.dram_tensor(f"in_{name}", a.shape, _mybir.dt.from_np(a.dtype), kind="ExternalInput").ap())
    args.append(nc.dram_tensor("out_0", (GRAPHS, NODES, D), _mybir.dt.float32, kind="ExternalOutput").ap())
    build(nc, *args)
    r = _run(nc, [arrays], core_ids=[0])
    return r.results[0]["out_0"]
```

```python
import concourse.bass as bass
from concourse import mybir
from contextlib import ExitStack

GRAPHS, NODES, D = 64, 128, 256
HEADS = 8
HD = D // HEADS
HIDDEN = 4 * D
PER = 4
GROUPS = GRAPHS // PER
TOK = PER * NODES
KT = D // 128
HT = HIDDEN // 128
HPT = 128 // HD
EPS = 1e-5
SCALE0 = 1.0 / float(HD) ** 0.5
SCALE1 = 1.0 / float(D) ** 0.5
MASKED = -1.0e30
CONSTS = 4
SPLIT = {n: i + 1 for i, n in enumerate(("wk", "wq", "wv", "wo", "w2", "w1", "qk1", "vo1"))}
ALL = slice(None)
CAT = 16 * 2 * HPT * 3
LN_STEPS = 14


def build(nc, x, adj, ln1_g, ln1_b, ln2_g, ln2_b, wq, bq, wk, bk, wv, bv, wo, bo, w1, b1, w2, b2,
          wq1, wk1, wv1, wo1, bo1, gamma, beta, out):
    f32, f32r, i32 = mybir.dt.float32, mybir.dt.float32r, mybir.dt.int32
    ALU, ACT = mybir.AluOpType, mybir.ActivationFunctionType

    x_v = x.rearrange("(g b) n d -> g n b d", b=PER)
    adj_v = adj.rearrange("(g b) q k -> g q b k", b=PER)
    out_v = out.rearrange("(g b) n d -> g n b d", b=PER)

    with ExitStack() as ctx:
        def sb(name, shape, dt=f32):
            return ctx.enter_context(nc.sbuf_tensor(name, shape, dt))

        def sem(name):
            return ctx.enter_context(nc.semaphore(name))

        def parts(name, shape):
            return sb(name + "_hi", shape, f32r), sb(name + "_lo", shape, f32r)

        wq_p, wk_p, wv_p, wo_p = (parts(n, [128, KT, D]) for n in ("wq", "wk", "wv", "wo"))
        w1_p = parts("w1", [128, KT, HIDDEN])
        w2_p = parts("w2", [128, HT, D])
        qk1_p = parts("qk1", [128, KT, D])
        vo1_p = parts("vo1", [128, KT, D])
        cols = {n: sb(n + "_c", [128, KT]) for n in ("ln1_g", "ln1_b", "ln2_g", "ln2_b", "bq", "bk", "bv")}
        b1_c = sb("b1_c", [128, HT])
        ln1_gs = sb("ln1_gs", [128, KT])
        rows = {n: sb(n + "_r", [128, D]) for n in ("bo", "b2", "bo1", "gamma", "beta")}
        ident = sb("ident", [128, 128])
        minus_half = sb("minus_half", [128, PER])
        gelu_probe = sb("gelu_probe", [128, 1])

        xs = sb("xs", [128, PER, D])
        adj_i = sb("adj_i", [128, PER, NODES], i32)
        adj_f = sb("adj_f", [128, PER, NODES])
        bias0 = sb("bias0", [128, PER, NODES])
        pen0 = adj_i[:, :, :].bitcast(f32)
        pen1 = sb("pen1", [128, PER, NODES])
        x_bo = sb("x_bo", [128, PER, D])
        nx = sb("nx", [128, PER, D])
        q_cat = sb("q_cat", [128, HEADS, TOK], f32r)
        k_cat = sb("k_cat", [128, HEADS, TOK], f32r)
        kT = parts("kT", [128, KT, TOK])
        v_one = sb("v_one", [128, PER, HEADS, HD + 1])
        p_s = sb("p_s", [128, 2, HEADS, NODES])
        neg_max = sb("neg_max", [128, 2, HEADS])
        pT = sb("pT", [128, 2, HEADS, NODES])
        rsum = sb("rsum", [128, 2, HEADS])
        attn = sb("attn", [128, 2, D])
        bv_cols = attn[:, 0, :].rearrange("p (t n) -> p t n", t=KT)
        attnT = parts("attnT", [128, 2, KT, NODES])
        x1 = sb("x1", [128, PER, D])
        n2T = parts("n2T", [128, KT, TOK])
        h_f = sb("h_f", [128, 2, TOK])
        hT = parts("hT", [128, HT, TOK])
        x2 = sb("x2", [128, PER, D])
        p1 = sb("p1", [128, PER, NODES])
        neg_max1 = sb("neg_max1", [128, PER])
        sum1 = sb("sum1", [128, PER])
        rsum1 = sb("rsum1", [128, PER])
        y = sb("y", [128, PER, D])
        x2T = [part[:, 0:KT, :] for part in hT]
        nxT = [part[:, KT:2 * KT, :] for part in hT]
        last_x2T = [q_cat[:, 0:KT, :], q_cat[:, KT:2 * KT, :]]
        x2T_f = p_s[:, 0, :, :].rearrange("p h n -> p (h n)").rearrange("p (t n) -> p t n", t=KT)
        tT = p_s[:, 1, :, :].rearrange("p h n -> p (h n)").rearrange("p (t n) -> p t n", t=KT)
        vo = pT[:, 0, :, :].rearrange("p h n -> p (h n)").rearrange("p (b d) -> p b d", b=PER)
        p1T = pT[:, 1, 0:PER, :]
        qT = [p_s[:, i, :, :].rearrange("p h n -> p (h n)").rearrange("p (t n) -> p t n", t=KT).bitcast(f32r)
              for i in range(2)]
        raw = {"wk": x1[:, 0:KT, :], "wq": x1[:, KT:2 * KT, :]}
        raw["wv"], raw["wo"] = (h_f[:, i, :].rearrange("p (t n) -> p t n", t=KT) for i in range(2))
        raw["w1"] = pT[:, :, :, :].rearrange("p a h n -> p (a h n)").rearrange("p (t n) -> p t n", t=KT)
        raw["w2"] = p_s[:, :, :, :].rearrange("p a h n -> p (a h n)").rearrange("p (t n) -> p t n", t=HT)
        raw["wq1"], raw["wk1"] = x2[:, 0:KT, :], x2[:, KT:2 * KT, :]
        raw["wv1"], raw["wo1"] = y[:, 0:KT, :], y[:, KT:2 * KT, :]
        l1_T = {"wq1": raw["wv"], "wk1": raw["wo"], "wv1": raw["wq1"]}
        lns = {n: dict(stats=sb(f"stats{n}", [128, PER, 6]), mv=sb(f"mv{n}", [128, PER, 2]),
                       ve=sb(f"ve{n}", [128, PER]), rstd=sb(f"rstd{n}", [128, PER]),
                       shift=sb(f"shift{n}", [128, PER])) for n in (1, 2, 3)}

        bank = [ctx.enter_context(nc.psum_tensor(f"bank{i}", [128, 512], f32)) for i in range(8)]

        w_load = {n: sem(f"{n}_load") for n in ("wk", "wq", "wv", "wo", "w1", "w2", "l1")}
        ln1_load, col_load, row_load = sem("ln1_load"), sem("col_load"), sem("row_load")
        x_load = sem("x_load")
        adj_load = sem("adj_load")
        out_store = sem("out_store")
        cat_load = sem("cat_load")
        consts = sem("consts")
        act_hi, dve_lo = sem("act_hi"), sem("dve_lo")
        pe_shift, dve_shift = sem("pe_shift"), sem("dve_shift")
        pe_l1, pe_l1_mm, dve_l1 = sem("pe_l1"), sem("pe_l1_mm"), sem("dve_l1")
        stand_dve, stand_pool = sem("stand_dve"), sem("stand_pool")
        pe_nxT = sem("pe_nxT")
        pe_k, pe_q, pe_v = sem("pe_k"), sem("pe_q"), sem("pe_v")
        pe_s, pe_pT, pe_av = sem("pe_s"), sem("pe_pT"), sem("pe_av")
        pe_attnT, pe_wo = sem("pe_attnT"), sem("pe_wo")
        pe_n2T = sem("pe_n2T")
        pe_up = sem("pe_up")
        pe_down = sem("pe_down")
        pe_x2T = sem("pe_x2T")
        pe_t, pe_vo = sem("pe_t"), sem("pe_vo")
        pe_s1, pe_p1T = sem("pe_s1"), sem("pe_p1T")
        pe_av1 = sem("pe_av1")
        act_nxT, act_k = sem("act_nxT"), sem("act_k")
        act_v = sem("act_v")
        act_q = sem("act_q")
        act_p = sem("act_p")
        act_pT, act_attnT = sem("act_pT"), sem("act_attnT")
        act_n2T = sem("act_n2T")
        act_h = sem("act_h")
        act_x2T, act_t, act_vo = sem("act_x2T"), sem("act_t"), sem("act_vo")
        act_p1 = sem("act_p1")
        ln_dve = {n: sem(f"ln{n}_dve") for n in (1, 2, 3)}
        dve_nxT, dve_k, dve_q = sem("dve_nxT"), sem("dve_k"), sem("dve_q")
        dve_s = sem("dve_s")
        dve_pT, dve_r, dve_attn = sem("dve_pT"), sem("dve_r"), sem("dve_attn")
        dve_x1 = sem("dve_x1")
        dve_attnT = sem("dve_attnT")
        dve_n2T = sem("dve_n2T")
        dve_h_hi, dve_h = sem("dve_h_hi"), sem("dve_h")
        dve_x2 = sem("dve_x2")
        dve_x2T_hi, dve_x2T = sem("dve_x2T_hi"), sem("dve_x2T")
        dve_t, dve_vo = sem("dve_t"), sem("dve_vo")
        dve_s1 = sem("dve_s1")
        dve_p1T, dve_r1 = sem("dve_p1T"), sem("dve_r1")
        dve_y = sem("dve_y")
        dve_out = sem("dve_out")
        ln_pool = {n: sem(f"ln{n}_pool") for n in (1, 2, 3)}
        pool_adj = sem("pool_adj")
        pool_bias = sem("pool_bias")
        pool_pen1 = sem("pool_pen1")
        pool_xbo, pool_x1b, pool_x2b = sem("pool_xbo"), sem("pool_x1b"), sem("pool_x2b")
        pool_out = sem("pool_out")

        weight_loads = [("wo", raw["wo"], wo), ("w2", raw["w2"], w2), ("w1", raw["w1"], w1),
                        ("l1", raw["wq1"], wq1), ("l1", raw["wk1"], wk1), ("l1", raw["wv1"], wv1), ("l1", raw["wo1"], wo1)]
        ln1_loads = [(cols["ln1_g"], ln1_g), (cols["ln1_b"], ln1_b)]
        col_loads = [(cols["bk"], bk), (cols["bq"], bq), (cols["bv"], bv), (cols["ln2_g"], ln2_g),
                     (cols["ln2_b"], ln2_b), (b1_c, b1)]
        row_loads = [(rows["bo"], bo), (rows["b2"], b2), (rows["bo1"], bo1), (rows["gamma"], gamma),
                     (rows["beta"], beta)]
        LN1_ALL, COLS_ALL, ROWS_ALL = 16 * len(ln1_loads), 16 * len(col_loads), 16 * len(row_loads)
        L1_ALL = 16 * sum(n == 'l1' for n, _, _ in weight_loads)

        block = ctx.enter_context(nc.Block())

        @block.sync
        def _(sp):
            def load_x(g):
                sp.wait_ge(ln_dve[1], LN_STEPS * g)
                sp.wait_ge(pool_xbo, g)
                sp.dma_start(xs[:, :, :], x_v[g]).then_inc(x_load, 16)

            def load_adj(g):
                sp.wait_ge(pool_bias, 4 * g)
                sp.dma_start(adj_i[:, :, :], adj_v[g]).then_inc(adj_load, 16)

            def load_weight(n, dst, src):
                sp.dma_start(dst, src.rearrange("(t p) n -> p t n", p=128)).then_inc(w_load[n], 16)

            def store(g):
                sp.wait_ge(pool_out, 2 * g + 2)
                sp.dma_start(out_v[g], y[:, :, :]).then_inc(out_store, 16)

            def stack(g):
                sp.wait_ge(pe_s, 4 * g)
                for cat, src, order, ready in ((k_cat, kT, (0, 1, 0), (act_k, dve_k)), (q_cat, qT, (0, 0, 1), (act_q, dve_q))):
                    for part in range(2):
                        sp.wait_ge(ready[part], 2 * g + 2)
                        for place in range(len(order)):
                            for r in range(HPT):
                                if order[place] == part:
                                    sp.dma_start(cat[HD * place:HD * place + HD, r:HEADS:HPT, :].bitcast(f32),
                                                 src[part][HD * r:HD * r + HD, :, :].bitcast(f32)).then_inc(cat_load, 16)

            load_x(0)
            for n, src in (("wk", wk), ("wq", wq), ("wv", wv)):
                load_weight(n, raw[n], src)
            load_adj(0)
            for n, dst, src in weight_loads:
                load_weight(n, dst, src)
            for dst, src in row_loads:
                sp.dma_start(dst[:, :], src.rearrange("(a d) -> a d", a=1).to_broadcast([128, D])).then_inc(row_load, 16)
            stack(0)
            load_x(1)
            load_adj(1)
            for g in (1, 2):
                stack(g)
                load_x(g + 1)
                load_adj(g + 1)
            with sp.Fori(3, GROUPS - 1) as g:
                store(g - 3)
                stack(g)
                load_x(g + 1)
                load_adj(g + 1)
            store(GROUPS - 4)
            stack(GROUPS - 1)
            for g in range(GROUPS - 3, GROUPS - 1):
                store(g)
            for half, finished, count in ((0, pool_out, 2 * GROUPS), (1, dve_out, 2)):
                b = slice(2 * half, 2 * half + 2)
                sp.wait_ge(finished, count)
                sp.dma_start(out_v[GROUPS - 1][:, b], y[:, b, :]).then_inc(out_store, 16)
            sp.wait_ge(out_store, 16 * (GROUPS + 1))

        @block.tensor
        def _(pe):
            mm, tr = nc.tensor.matmul, nc.tensor.transpose

            def mm3(out, a, b, first=True, last=True):
                (a_hi, a_lo), (b_hi, b_lo) = a, b
                mm(out, a_hi, b_hi, start=first, stop=False)
                mm(out, a_hi, b_lo, start=False, stop=False)
                return mm(out, a_lo, b_hi, start=False, stop=last)

            def both(p, *index):
                return [part[index] for part in p]

            def shift_columns(dst, w, b, cols_out):
                for m in range(cols_out):
                    for t in range(KT):
                        last = mm(dst[:, m:m + 1], w[:, t, 128 * m:128 * m + 128], b[:, t:t + 1],
                                  start=(t == 0), stop=(t == KT - 1))
                return last

            def shifts_kq():
                pe.wait_ge(ln1_load, LN1_ALL)
                for i, n in enumerate(("wk", "wq")):
                    pe.wait_ge(w_load[n], 16)
                    last = shift_columns(bank[6][:, KT * i:KT * i + KT], raw[n], cols["ln1_b"], KT)
                last.then_inc(pe_shift, 1)

            def shift_v():
                pe.wait_ge(w_load["wv"], 16)
                shift_columns(bank[7][:, 0:KT], raw["wv"], cols["ln1_b"], KT).then_inc(pe_shift, 1)

            def shift_bo():
                pe.wait_ge(dve_shift, 6)
                pe.wait_ge(w_load["wo"], 16)
                for t in range(KT):
                    last = mm(bank[7][:, 0:D], bv_cols[:, t, :], raw["wo"][:, t, :], start=(t == 0), stop=(t == KT - 1))
                last.then_inc(pe_shift, 1)

            def shifts_up():
                pe.wait_ge(dve_shift, 3)
                pe.wait_ge(w_load["w1"], 16)
                pe.wait_ge(col_load, COLS_ALL)
                shift_columns(bank[6], raw["w1"], cols["ln2_b"], HT).then_inc(pe_shift, 1)

            def l1_transpose(i):
                pe.wait_ge(w_load["l1"], L1_ALL)
                pe.wait_ge(dve_shift, 8)
                if i == 2:
                    pe.wait_ge(dve_l1, 1)
                for c in range(KT):
                    for r in range(KT):
                        last = tr(bank[7 - i % 2][:, D * c + 128 * r:D * c + 128 * r + 128],
                                  raw[("wq1", "wk1", "wv1")[i]][:, r, 128 * c:128 * c + 128], ident[:, :])
                last.then_inc(pe_l1, 1)

            def l1_product(k):
                pe.wait_ge(dve_l1, 2 + k)
                n, rhs = (("wq1", l1_T["wk1"]), ("wv1", raw["wo1"]))[k]
                for m in range(KT):
                    for c in range(KT):
                        last = mm(bank[6 + k][:, D * m:D * m + D], l1_T[n][:, c, 128 * m:128 * m + 128],
                                  rhs[:, c, :], start=(c == 0), stop=(c == KT - 1))
                last.then_inc(pe_l1_mm, 1)

            def nodes(b):
                return slice(128 * b, 128 * b + 128)

            def norm_transpose(g):
                pe.wait_ge(ln_dve[1], LN_STEPS * g + LN_STEPS)
                pe.wait_ge(act_pT, 4 * g)
                pe.wait_ge(dve_pT, 4 * g)
                for t in range(KT):
                    for b in range(PER):
                        last = tr(bank[2 + t][:, nodes(b)], nx[:, b, 128 * t:128 * t + 128], ident[:, :])
                    last.then_inc(pe_nxT, 1)

            def project_k(g, m):
                pe.wait_ge(dve_nxT, 2 * g + 2)
                for t in range(KT):
                    last = mm3(bank[2 + m][:, :], both(wk_p, ALL, t, nodes(m)), both(nxT, ALL, t),
                               t == 0, t == KT - 1)
                last.then_inc(pe_k, 1)

            def project_q(g, m):
                pe.wait_ge(dve_s, 8 * g)
                for t in range(KT):
                    last = mm3(bank[m][:, :], both(wq_p, ALL, t, nodes(m)), both(nxT, ALL, t),
                               t == 0, t == KT - 1)
                last.then_inc(pe_q, 1)

            def project_v(g, halves=range(2)):
                pe.wait_ge(dve_attn, 4 * g)
                pe.wait_ge(dve_x1, 4 * g)
                for half in halves:
                    for b in (2 * half, 2 * half + 1):
                        for t in range(KT):
                            last = mm3(bank[4 + half][:, D * (b % 2):D * (b % 2) + D],
                                       both(nxT, ALL, t, nodes(b)), both(wv_p, ALL, t), t == 0, t == KT - 1)
                    last.then_inc(pe_v, 1)

            def scores(g, b):
                if b == 0:
                    pe.wait_ge(cat_load, CAT * g + CAT)
                else:
                    pe.wait_ge(dve_s, 8 * g + 2 * b)
                for h in range(HEADS):
                    last = mm(bank[h // HPT][:, nodes(h % HPT)], q_cat[0:3 * HD, h, nodes(b)],
                              k_cat[0:3 * HD, h, nodes(b)], start=True, stop=True)
                last.then_inc(pe_s, 1)

            def p_transpose(g, b):
                if b > 0:
                    pe.wait_ge(act_pT, 4 * g + b)
                    pe.wait_ge(dve_pT, 4 * g + b)
                for h in range(HEADS):
                    if h % HPT == 0:
                        pe.wait_ge(act_p, 8 * g + 2 * b + h // HPT + 1)
                    last = tr(bank[2 + h // HPT][:, nodes(h % HPT)], p_s[:, b % 2, h, :], ident[:, :])
                last.then_inc(pe_pT, 1)

            def attend(g, b):
                pe.wait_ge(act_pT, 4 * g + b + 1)
                pe.wait_ge(dve_pT, 4 * g + b + 1)
                pe.wait_ge(act_v, 2 * g + 2)
                pe.wait_ge(dve_attn, 4 * g + b)
                for h in range(HEADS):
                    last = mm(bank[4][:, (HD + 1) * h:(HD + 1) * (h + 1)], pT[:, b % 2, h, :],
                              v_one[:, b, h, :], start=True, stop=True)
                last.then_inc(pe_av, 1)

            def attn_transpose(g, b):
                pe.wait_ge(dve_attn, 4 * g + b + 1)
                pe.wait_ge(dve_x1, 4 * g + b)
                for t in range(KT):
                    last = tr(bank[5][:, nodes(t)], attn[:, b % 2, 128 * t:128 * t + 128], ident[:, :])
                last.then_inc(pe_attnT, 1)

            def out_project(g, b):
                pe.wait_ge(dve_attnT, 4 * g + b + 1)
                for t in range(KT):
                    last = mm3(bank[5][:, 0:D], both(attnT, ALL, b % 2, t), both(wo_p, ALL, t), t == 0, t == KT - 1)
                last.then_inc(pe_wo, 1)

            def n2_transpose(g, first_bank):
                pe.wait_ge(ln_dve[2], LN_STEPS * g + LN_STEPS)
                if first_bank == 6:
                    pe.wait_ge(dve_y, 4 * g)
                else:
                    pe.wait_ge(act_pT, 4 * g + 4)
                    pe.wait_ge(dve_pT, 4 * g + 4)
                for t in range(KT):
                    for b in range(PER):
                        last = tr(bank[first_bank + t][:, nodes(b)], nx[:, b, 128 * t:128 * t + 128], ident[:, :])
                    last.then_inc(pe_n2T, 1)

            def mlp_up(g, j):
                if j == 0:
                    pe.wait_ge(dve_n2T, 2 * g + 2)
                elif j >= 2:
                    pe.wait_ge(act_h, HT * g + j - 1)
                for t in range(KT):
                    last = mm3(bank[6 + j % 2][:, :], both(w1_p, ALL, t, nodes(j)), both(n2T, ALL, t),
                               t == 0, t == KT - 1)
                last.then_inc(pe_up, 1)

            def mlp_down(g, b):
                if b < 2:
                    pe.wait_ge(act_h, HT * g + HT - 1 + b)
                else:
                    pe.wait_ge(dve_x2, 4 * g + b - 1)
                for j in range(HT):
                    if b == 0:
                        pe.wait_ge(dve_h, HT * g + j + 1)
                    last = mm3(bank[6 + b % 2][:, 0:D], both(hT, ALL, j, nodes(b)), both(w2_p, ALL, j),
                               j == 0, j == HT - 1)
                last.then_inc(pe_down, 1)

            def x2_transpose(g):
                pe.wait_ge(dve_x2, 4 * g + 4)
                for t in range(KT):
                    for b in range(PER):
                        last = tr(bank[6 + t][:, nodes(b)], x2[:, b, 128 * t:128 * t + 128], ident[:, :])
                    last.then_inc(pe_x2T, 1)

            def last_x2_transpose(b):
                pe.wait_ge(dve_x2, 4 * (GROUPS - 1) + b + 1)
                for t in range(KT):
                    last = tr(bank[2 + b][:, nodes(t)], x2[:, b, 128 * t:128 * t + 128], ident[:, :])
                last.then_inc(pe_x2T, 1)

            def t_project(g, x2T, steps):
                pe.wait_ge(dve_x2T, 2 * g + steps)
                for m in range(KT):
                    for t in range(KT):
                        last = mm3(bank[6 + m][:, :], both(qk1_p, ALL, t, nodes(m)), both(x2T, ALL, t),
                                   t == 0, t == KT - 1)
                    last.then_inc(pe_t, 1)

            def scores1(g):
                pe.wait_ge(act_t, g + 1)
                pe.wait_ge(dve_t, g + 1)
                for b in range(PER):
                    for t in range(KT):
                        last = mm(bank[6][:, nodes(b)], tT[:, t, nodes(b)], x2T_f[:, t, nodes(b)],
                                  start=(t == 0), stop=(t == KT - 1))
                last.then_inc(pe_s1, 1)

            def vo_project(g, half, x2T):
                if half == 1:
                    pe.wait_ge(dve_s1, g + 1)
                for b in (2 * half, 2 * half + 1):
                    for t in range(KT):
                        last = mm3(bank[7 - half][:, D * (b % 2):D * (b % 2) + D], both(x2T, ALL, t, nodes(b)),
                                   both(vo1_p, ALL, t), t == 0, t == KT - 1)
                last.then_inc(pe_vo, 1)

            def p1_transpose(g):
                pe.wait_ge(act_p1, 4 * g + 4)
                for b in range(PER):
                    last = tr(bank[4][:, nodes(b)], p1[:, b, :], ident[:, :])
                last.then_inc(pe_p1T, 1)

            def attend1(g):
                pe.wait_ge(dve_p1T, g + 1)
                pe.wait_ge(act_vo, g + 1)
                pe.wait_ge(dve_vo, g + 1)
                for half in range(2):
                    for b in (2 * half, 2 * half + 1):
                        last = mm(bank[6 + half][:, 256 * (b % 2):256 * (b % 2) + 256], p1T[:, b, :], vo[:, b, :],
                                  start=True, stop=True)
                    last.then_inc(pe_av1, 1)

            def turn(gp, ga, gb):
                P, A, B = gp is not None, ga is not None, gb is not None
                xT, steps = (x2T, KT) if A else (last_x2T, PER)
                if B:
                    for j in range(HT):
                        mlp_up(gb, j)
                for k in range(PER + 1):
                    if A and k < PER:
                        scores(ga, k)
                    if A and k >= 1:
                        p_transpose(ga, k - 1)
                    if A and k >= 2:
                        attn_transpose(ga, k - 2)
                    if B and k < PER:
                        mlp_down(gb, k)
                    if B and A and k == PER:
                        x2_transpose(gb)
                    if B and not A and k >= 1:
                        last_x2_transpose(k - 1)
                    if A and k >= 1:
                        attend(ga, k - 1)
                    if A and k >= 2:
                        out_project(ga, k - 2)
                if P:
                    norm_transpose(gp)
                if B:
                    t_project(gb, xT, steps)
                if A:
                    attn_transpose(ga, PER - 1)
                if P:
                    project_k(gp, 0)
                if A and not B:
                    out_project(ga, PER - 1)
                if P:
                    project_k(gp, 1)
                if B:
                    scores1(gb)
                if A and B:
                    out_project(ga, PER - 1)
                if B:
                    vo_project(gb, 0, xT)
                    vo_project(gb, 1, xT)
                    p1_transpose(gb)
                if P:
                    project_q(gp, 0)
                if B:
                    attend1(gb)
                if P:
                    project_q(gp, 1)
                if P and not B:
                    project_v(gp, [0])
                if A:
                    n2_transpose(ga, 6 if P else 2)
                if P:
                    project_v(gp, range(2) if B else [1])

            shifts_kq()
            pe.wait_ge(consts, CONSTS)
            norm_transpose(0)
            shift_v()
            for m in range(KT):
                pe.wait_ge(dve_lo, SPLIT["wk"])
                project_k(0, m)
            pe.wait_ge(dve_lo, SPLIT["wq"])
            project_q(0, 0)
            project_q(0, 1)
            shift_bo()
            pe.wait_ge(dve_lo, SPLIT["wv"])
            project_v(0)
            shifts_up()
            for i in range(3):
                l1_transpose(i)
            for k in range(2):
                l1_product(k)
            turn(1, 0, None)
            turn(2, 1, 0)
            with pe.Fori(2, GROUPS - 1) as g:
                turn(g + 1, g, g - 1)
            turn(None, GROUPS - 1, GROUPS - 2)
            turn(None, None, GROUPS - 1)

        @block.scalar
        def _(act):
            run = nc.scalar.activation
            for loads, loaded in ((ln1_loads, ln1_load), (col_loads, col_load)):
                for dst, src in loads:
                    with nc.allow_non_contiguous_dma(reason="a bias vector onto partitions"):
                        act.dma_start(dst[:, :], src.rearrange("(t p) -> p t", p=128)).then_inc(loaded, 16)

            def identity(dst, src, **kw):
                return run(dst, src, ACT.Identity, **kw)

            def high(n, w, gain=None):
                act.wait_ge(w_load[n], 16)
                if gain is None:
                    last = run(w[0][:, :, :], raw[n], ACT.Copy)
                else:
                    for t in range(KT):
                        last = run(w[0][:, t, :], raw[n][:, t, :], ACT.Copy, scale=gain[:, t:t + 1])
                last.then_inc(act_hi, 1)

            def layer1_high():
                for k, (w, scale) in enumerate(((qk1_p, SCALE1), (vo1_p, 1.0))):
                    act.wait_ge(pe_l1_mm, 1 + k)
                    run(w[0][:, :, :], bank[6 + k][:, :].rearrange("p (m d) -> p m d", m=KT), ACT.Copy,
                        scale=scale).then_inc(act_hi, 1)

            def nxT_copy(g):
                for t in range(KT):
                    act.wait_ge(pe_nxT, 2 * g + t + 1)
                    identity(nxT[0][:, t, :], bank[2 + t][:, :]).then_inc(act_nxT, 1)

            def k_copy(g, t):
                act.wait_ge(pe_k, 2 * g + t + 1)
                run(kT[0][:, t, :], bank[2 + t][:, :], ACT.Identity, bias=cols["bk"][:, t:t + 1]).then_inc(act_k, 1)

            def q_copy(g):
                for t in range(KT):
                    act.wait_ge(pe_q, 2 * g + t + 1)
                    run(qT[0][:, t, :], bank[t][:, :], ACT.Identity, bias=cols["bq"][:, t:t + 1]).then_inc(act_q, 1)

            def v_copy(g):
                act.wait_ge(pe_av, 4 * g)
                for half in range(2):
                    act.wait_ge(pe_v, 2 * g + half + 1)
                    identity(v_one[:, 2 * half:2 * half + 2, :, 0:HD],
                             bank[4 + half][:, :].rearrange("p (b h d) -> p b h d", b=2, h=HEADS)).then_inc(act_v, 1)

            def exps(g, b):
                for h in range(HEADS):
                    if h % HPT == 0:
                        act.wait_ge(dve_s, 8 * g + 2 * b + h // HPT + 1)
                    last = run(p_s[:, b % 2, h, :], p_s[:, b % 2, h, :], ACT.Exp, scale=-1.0,
                               bias=neg_max[:, b % 2, h:h + 1])
                    if h % HPT == HPT - 1:
                        last.then_inc(act_p, 1)

            def pT_copy(g, b):
                act.wait_ge(pe_pT, 4 * g + b + 1)
                act.wait_ge(pe_av, 4 * g + max(b - 1, 0))
                run(pT[:, b % 2, 0:HPT, :], bank[2][:, :].rearrange("p (h n) -> p h n", h=HPT),
                    ACT.Identity).then_inc(act_pT, 1)

            def attnT_copy(g, b):
                act.wait_ge(pe_attnT, 4 * g + b + 1)
                act.wait_ge(pe_wo, 4 * g + max(b - 1, 0))
                run(attnT[0][:, b % 2, :, :], bank[5][:, 0:D].rearrange("p (t n) -> p t n", t=KT),
                    ACT.Identity).then_inc(act_attnT, 1)

            def n2T_copy(g, first_bank):
                for t in range(KT):
                    act.wait_ge(pe_n2T, 2 * g + t + 1)
                    identity(n2T[0][:, t, :], bank[first_bank + t][:, :]).then_inc(act_n2T, 1)

            def gelu(g, j):
                act.wait_ge(pe_up, HT * g + j + 1)
                act.wait_ge(dve_h, HT * g + max(j - 1, 0))
                run(h_f[:, j % 2, :], bank[6 + j % 2][:, :], ACT.Gelu, bias=b1_c[:, j:j + 1]).then_inc(act_h, 1)

            def x2T_copy(g):
                for t in range(KT):
                    act.wait_ge(pe_x2T, 2 * g + t + 1)
                    identity(x2T_f[:, t, :], bank[6 + t][:, :]).then_inc(act_x2T, 1)

            def last_x2T_copy(b):
                act.wait_ge(pe_x2T, 2 * (GROUPS - 1) + b + 1)
                identity(x2T_f[:, :, NODES * b:NODES * b + NODES],
                         bank[2 + b][:, 0:D].rearrange("p (t n) -> p t n", t=KT)).then_inc(act_x2T, 1)

            def t_copy(g):
                act.wait_ge(pe_t, 2 * g + 1)
                run(tT[:, 0, :], bank[6][:, :], ACT.Identity).then_inc(act_t, 1)

            def exps1(g):
                act.wait_ge(dve_s1, g + 1)
                act.wait_ge(dve_r1, g)
                for b in range(PER):
                    run(p1[:, b, :], p1[:, b, :], ACT.Exp, scale=-1.0, bias=neg_max1[:, b:b + 1],
                        accum_out=sum1[:, b:b + 1]).then_inc(act_p1, 1)

            def vo_copy(g):
                act.wait_ge(pe_vo, 2 * g + 1)
                run(vo[:, 0:2, :], bank[7][:, :].rearrange("p (b d) -> p b d", b=2), ACT.Identity).then_inc(act_vo, 1)

            def turn(gp, ga, gb):
                P, A, B = gp is not None, ga is not None, gb is not None
                if B:
                    for j in range(HT):
                        gelu(gb, j)
                for k in range(PER + 1):
                    if A and k >= 1:
                        pT_copy(ga, k - 1)
                    if A and k >= 2:
                        attnT_copy(ga, k - 2)
                    if A and k < PER:
                        exps(ga, k)
                if B and A:
                    x2T_copy(gb)
                if B and not A:
                    for b in range(PER):
                        last_x2T_copy(b)
                if P:
                    nxT_copy(gp)
                if B:
                    t_copy(gb)
                if A:
                    attnT_copy(ga, PER - 1)
                if P:
                    k_copy(gp, 0)
                    k_copy(gp, 1)
                if B:
                    exps1(gb)
                    vo_copy(gb)
                if A:
                    run(gelu_probe[:, :], minus_half[:, 0:1], ACT.Gelu)
                if P:
                    q_copy(gp)
                if A:
                    n2T_copy(ga, 6 if P else 2)
                if P:
                    v_copy(gp)

            act.wait_ge(consts, 3)
            run(gelu_probe[:, :], minus_half[:, 0:1], ACT.Copy)
            act.wait_ge(ln1_load, LN1_ALL)
            high("wk", wk_p, cols["ln1_g"])
            act.wait_ge(dve_shift, 1)
            high("wq", wq_p, ln1_gs)
            nxT_copy(0)
            high("wv", wv_p, cols["ln1_g"])
            high("wo", wo_p)
            act.wait_ge(dve_shift, 4)
            high("w2", w2_p)
            k_copy(0, 0)
            k_copy(0, 1)
            act.wait_ge(dve_lo, SPLIT["w2"])
            q_copy(0)
            v_copy(0)
            act.wait_ge(col_load, COLS_ALL)
            high("w1", w1_p, cols["ln2_g"])
            layer1_high()
            act.wait_ge(dve_lo, SPLIT["w1"])
            turn(1, 0, None)
            turn(2, 1, 0)
            with act.Fori(2, GROUPS - 1) as g:
                turn(g + 1, g, g - 1)
            turn(None, GROUPS - 1, GROUPS - 2)
            turn(None, None, GROUPS - 1)

        @block.vector
        def _(dve):
            V = nc.vector
            V.memset(v_one[:, :, :, :], 1.0).then_inc(consts, 1)
            V.memset(minus_half[:, :], -0.5).then_inc(consts, 1)

            def low(dst, src, hi, gain=None):
                if gain is None:
                    return V.tensor_tensor(dst, src, hi.bitcast(f32), ALU.subtract)
                return V.scalar_tensor_tensor(out=dst, in0=src, scalar=gain, in1=hi.bitcast(f32),
                                              op0=ALU.mult, op1=ALU.subtract)

            def shifts_kq():
                dve.wait_ge(col_load, COLS_ALL)
                dve.wait_ge(pe_shift, 1)
                V.tensor_tensor(cols["bk"][:, :], bank[6][:, 0:KT], cols["bk"][:, :], ALU.add).then_inc(dve_shift, 1)
                V.tensor_tensor(cols["bq"][:, :], bank[6][:, KT:2 * KT], cols["bq"][:, :], ALU.add).then_inc(dve_shift, 1)
                dve.wait_ge(dve_shift, 3)
                V.tensor_scalar(cols["bq"][:, :], cols["bq"][:, :], SCALE0, None, ALU.mult).then_inc(dve_shift, 1)

            def shift_v():
                dve.wait_ge(pe_shift, 2)
                V.tensor_tensor(cols["bv"][:, :], bank[7][:, 0:KT], cols["bv"][:, :], ALU.add).then_inc(dve_shift, 1)
                dve.wait_ge(dve_shift, 5)
                V.tensor_copy(bv_cols, cols["bv"][:, :, None].to_broadcast([128, KT, 128])).then_inc(dve_shift, 1)

            def shift_bo():
                dve.wait_ge(pe_shift, 3)
                dve.wait_ge(row_load, ROWS_ALL)
                V.tensor_tensor(rows["bo"][:, :], bank[7][:, 0:D], rows["bo"][:, :], ALU.add).then_inc(dve_shift, 1)

            def shifts_up():
                dve.wait_ge(pe_shift, 4)
                V.tensor_tensor(b1_c[:, :], bank[6][:, 0:HT], b1_c[:, :], ALU.add).then_inc(dve_shift, 1)

            def low_weight(n, w, gain=None):
                dve.wait_ge(act_hi, SPLIT[n])
                if gain is None:
                    last = low(w[1][:, :, :], raw[n], w[0][:, :, :])
                else:
                    for t in range(KT):
                        last = low(w[1][:, t, :], raw[n][:, t, :], w[0][:, t, :], gain[:, t:t + 1])
                last.then_inc(dve_lo, 1)

            def l1_copy(i, n):
                dve.wait_ge(pe_l1, 1 + i)
                if i == 0:
                    dve.wait_ge(dve_lo, SPLIT["wo"])
                V.tensor_copy(l1_T[n], bank[7 - i % 2][:, :].rearrange("p (c d) -> p c d", c=KT)).then_inc(dve_l1, 1)

            def l1_low(k, n, w, scale):
                dve.wait_ge(act_hi, SPLIT[n])
                low(w[1][:, :, :], bank[6 + k][:, :].rearrange("p (m d) -> p m d", m=KT), w[0][:, :, :],
                    scale).then_inc(dve_lo, 1)

            def moments(n, g, src):
                t, s, base = lns[n], ln_dve[n], LN_STEPS * g
                for b in range(PER):
                    V.bn_stats(t["stats"][:, b, :], src[:, b, :]).then_inc(s, 1)
                dve.wait_ge(s, base + 4)
                dve.sem_inc(stand_dve, 1)
                for b in range(PER):
                    V.bn_aggr(t["mv"][:, b, :], t["stats"][:, b, :]).then_inc(s, 1)
                dve.wait_ge(s, base + 8)
                dve.wait_ge(ln_pool[n], g)
                V.tensor_scalar(t["ve"][:, :], t["mv"][:, :, 1], EPS, None, ALU.add).then_inc(s, 1)

            def normed(n, g, src, dst):
                t, s, base = lns[n], ln_dve[n], LN_STEPS * g
                dve.wait_ge(ln_pool[n], g + 1)
                V.scalar_tensor_tensor(out=t["shift"][:, :], in0=t["mv"][:, :, 0], scalar=-1.0, in1=t["rstd"][:, :],
                                       op0=ALU.mult, op1=ALU.mult).then_inc(s, 1)
                dve.wait_ge(s, base + 10)
                for b in range(PER):
                    V.tensor_scalar(dst[:, b, :], src[:, b, :], t["rstd"][:, b:b + 1], t["shift"][:, b:b + 1],
                                    ALU.mult, ALU.add).then_inc(s, 1)

            def moments1(g):
                dve.wait_ge(x_load, 16 * g + 16)
                moments(1, g, xs)

            def norm1(g, first=False):
                if not first:
                    dve.wait_ge(pe_n2T, 2 * g - 2)
                normed(1, g, xs, nx)

            def nxT_low(g):
                for t in range(KT):
                    dve.wait_ge(act_nxT, 2 * g + t + 1)
                    low(nxT[1][:, t, :], bank[2 + t][:, :], nxT[0][:, t, :]).then_inc(dve_nxT, 1)

            def low_biased(dst, src, bias, hi):
                return V.scalar_tensor_tensor(out=dst, in0=src, scalar=bias, in1=hi.bitcast(f32),
                                              op0=ALU.add, op1=ALU.subtract)

            def k_low(g, t):
                dve.wait_ge(act_k, 2 * g + t + 1)
                low_biased(kT[1][:, t, :], bank[2 + t][:, :], cols["bk"][:, t:t + 1], kT[0][:, t, :]).then_inc(dve_k, 1)

            def q_low(g, t):
                dve.wait_ge(act_q, 2 * g + t + 1)
                low_biased(qT[1][:, t, :], bank[t][:, :], cols["bq"][:, t:t + 1], qT[0][:, t, :]).then_inc(dve_q, 1)

            def biased(g, b):
                dve.wait_ge(pe_s, 4 * g + b + 1)
                if b == 0:
                    dve.wait_ge(pool_bias, 4 * g + 4)
                dve.wait_ge(pe_pT, 4 * g + max(b - 1, 0))
                dve.sem_inc(stand_dve, 1)
                for half in range(2):
                    for h in range(HPT * half, HPT * half + HPT):
                        last = V.tensor_tensor_reduce(
                            p_s[:, b % 2, h, :], bank[half][:, NODES * (h % HPT):NODES * (h % HPT) + NODES],
                            bias0[:, b, :], -1.0, -3.0 * MASKED, ALU.add, ALU.min, neg_max[:, b % 2, h:h + 1])
                    last.then_inc(dve_s, 1)

            def pT_copy(g, b):
                dve.wait_ge(pe_pT, 4 * g + b + 1)
                dve.wait_ge(pe_av, 4 * g + max(b - 1, 0))
                V.tensor_copy(pT[:, b % 2, HPT:HEADS, :],
                              bank[3][:, :].rearrange("p (h n) -> p h n", h=HPT)).then_inc(dve_pT, 1)

            def normalise(g, b):
                dve.wait_ge(pe_av, 4 * g + b + 1)
                dve.wait_ge(pe_attnT, 4 * g + max(b - 1, 0))
                av = bank[4][:, 0:HEADS * (HD + 1)].rearrange("p (h d) -> p h d", h=HEADS)
                V.reciprocal(rsum[:, b % 2, :], av[:, :, HD]).then_inc(dve_r, 1)
                dve.wait_ge(dve_r, 4 * g + b + 1)
                V.tensor_tensor(attn[:, b % 2, :].rearrange("p (h d) -> p h d", h=HEADS), av[:, :, 0:HD],
                                rsum[:, b % 2, :, None].to_broadcast([128, HEADS, HD]), ALU.mult).then_inc(dve_attn, 1)

            def residual1(g, b, first=False):
                dve.wait_ge(pe_wo, 4 * g + b + 1)
                if b == 0:
                    dve.wait_ge(pool_xbo, g + 1)
                if not first:
                    dve.wait_ge(dve_x2, 4 * g + b - 3)
                V.tensor_tensor(x1[:, b, :], bank[5][:, 0:D], x_bo[:, b, :], ALU.add).then_inc(dve_x1, 1)

            def moments2(g):
                dve.wait_ge(dve_x1, 4 * g + 4)
                moments(2, g, x1)

            def norm2(g):
                normed(2, g, x1, nx)

            def attnT_low(g, b):
                dve.wait_ge(act_attnT, 4 * g + b + 1)
                dve.wait_ge(pe_wo, 4 * g + max(b - 1, 0))
                low(attnT[1][:, b % 2, :, :], bank[5][:, 0:D].rearrange("p (t n) -> p t n", t=KT),
                    attnT[0][:, b % 2, :, :]).then_inc(dve_attnT, 1)

            def n2T_low(g, first_bank):
                for t in range(KT):
                    dve.wait_ge(act_n2T, 2 * g + t + 1)
                    low(n2T[1][:, t, :], bank[first_bank + t][:, :], n2T[0][:, t, :]).then_inc(dve_n2T, 1)

            def h_split(g, j):
                dve.wait_ge(act_h, HT * g + j + 1)
                V.tensor_copy(hT[0][:, j, :], h_f[:, j % 2, :]).then_inc(dve_h_hi, 1)
                dve.wait_ge(dve_h_hi, HT * g + j + 1)
                low(hT[1][:, j, :], h_f[:, j % 2, :], hT[0][:, j, :]).then_inc(dve_h, 1)

            def residual2(g, b):
                dve.wait_ge(pe_down, 4 * g + b + 1)
                if b == 0:
                    dve.wait_ge(pool_x1b, g + 1)
                    dve.wait_ge(dve_y, 4 * g)
                V.tensor_tensor(x2[:, b, :], bank[6 + b % 2][:, 0:D], x1[:, b, :], ALU.add).then_inc(dve_x2, 1)

            def x2T_split(g):
                for t in range(KT):
                    dve.wait_ge(act_x2T, 2 * g + t + 1)
                    V.tensor_copy(x2T[0][:, t, :], x2T_f[:, t, :]).then_inc(dve_x2T_hi, 1)
                    dve.wait_ge(dve_x2T_hi, 2 * g + t + 1)
                    low(x2T[1][:, t, :], x2T_f[:, t, :], x2T[0][:, t, :]).then_inc(dve_x2T, 1)

            def last_x2T_split(b):
                count, n = 2 * (GROUPS - 1) + b + 1, slice(NODES * b, NODES * b + NODES)
                dve.wait_ge(act_x2T, count)
                V.tensor_copy(last_x2T[0][:, :, n], x2T_f[:, :, n]).then_inc(dve_x2T_hi, 1)
                dve.wait_ge(dve_x2T_hi, count)
                low(last_x2T[1][:, :, n], x2T_f[:, :, n], last_x2T[0][:, :, n]).then_inc(dve_x2T, 1)

            def t_copy(g):
                dve.wait_ge(pe_t, 2 * g + 2)
                V.tensor_copy(tT[:, 1, :], bank[7][:, :]).then_inc(dve_t, 1)

            def biased1(g):
                dve.wait_ge(pe_s1, g + 1)
                dve.wait_ge(pool_pen1, g + 1)
                dve.wait_ge(pe_p1T, g)
                dve.sem_inc(stand_dve, 1)
                for b in range(PER):
                    last = V.tensor_tensor_reduce(p1[:, b, :], bank[6][:, NODES * b:NODES * b + NODES],
                                                  pen1[:, b, :], -1.0, -3.0 * MASKED, ALU.add, ALU.min, neg_max1[:, b:b + 1])
                last.then_inc(dve_s1, 1)

            def vo_copy(g):
                dve.wait_ge(pe_vo, 2 * g + 2)
                V.tensor_copy(vo[:, 2:4, :], bank[6][:, :].rearrange("p (b d) -> p b d", b=2)).then_inc(dve_vo, 1)

            def p1T_copy(g):
                dve.wait_ge(pe_p1T, g + 1)
                V.tensor_copy(p1T, bank[4][:, :].rearrange("p (b n) -> p b n", b=PER)).then_inc(dve_p1T, 1)
                dve.wait_ge(act_p1, 4 * g + 4)
                V.reciprocal(rsum1[:, :], sum1[:, :]).then_inc(dve_r1, 1)

            def residual3(g):
                dve.wait_ge(dve_r1, g + 1)
                dve.wait_ge(pool_x2b, g + 1)
                dve.wait_ge(out_store, 16 * g)
                for b in range(PER):
                    if b % 2 == 0:
                        dve.wait_ge(pe_av1, 2 * g + b // 2 + 1)
                    V.scalar_tensor_tensor(out=y[:, b, :], in0=bank[6 + b // 2][:, D * (b % 2):D * (b % 2) + D],
                                           scalar=rsum1[:, b:b + 1], in1=x2[:, b, :],
                                           op0=ALU.mult, op1=ALU.add).then_inc(dve_y, 1)

            def moments3(g):
                dve.wait_ge(dve_y, 4 * g + 4)
                moments(3, g, y)

            def norm3(g):
                normed(3, g, y, y)

            def finish_last():
                half = y[:, 2:4, :]
                dve.wait_ge(ln_dve[3], LN_STEPS * GROUPS)
                V.tensor_tensor(half, half, rows["gamma"][:, None, :].to_broadcast([128, 2, D]), ALU.mult).then_inc(dve_out, 1)
                dve.wait_ge(dve_out, 1)
                V.tensor_tensor(half, half, rows["beta"][:, None, :].to_broadcast([128, 2, D]), ALU.add).then_inc(dve_out, 1)

            def turn(gp, ga, gb, gc):
                P, A, B, C = gp is not None, ga is not None, gb is not None, gc is not None
                if B:
                    for j in range(HT):
                        h_split(gb, j)
                for k in range(PER + 1):
                    if A and k >= 1:
                        pT_copy(ga, k - 1)
                    if A and k < PER:
                        biased(ga, k)
                    if A and k >= 2:
                        attnT_low(ga, k - 2)
                    if P and k == 0:
                        moments1(gp)
                    if C and k == 1:
                        moments3(gc)
                    if B and k < PER:
                        residual2(gb, k)
                    if B and A and k == PER:
                        x2T_split(gb)
                    if B and not A and k >= 1:
                        last_x2T_split(k - 1)
                    if A and k >= 1:
                        normalise(ga, k - 1)
                    if A and k >= 2:
                        residual1(ga, k - 2, not B)
                    if P and k == 1:
                        norm1(gp)
                    if C and k == 2:
                        norm3(gc)
                if P:
                    nxT_low(gp)
                if B:
                    t_copy(gb)
                if A:
                    attnT_low(ga, PER - 1)
                if P and B:
                    k_low(gp, 0)
                    k_low(gp, 1)
                if B:
                    biased1(gb)
                if A:
                    residual1(ga, PER - 1, not B)
                    moments2(ga)
                if P and not B:
                    k_low(gp, 0)
                    k_low(gp, 1)
                if B:
                    vo_copy(gb)
                    p1T_copy(gb)
                if A:
                    norm2(ga)
                if B:
                    residual3(gb)
                if A:
                    n2T_low(ga, 6 if P else 2)
                if P:
                    q_low(gp, 0)
                    q_low(gp, 1)

            moments1(0)
            dve.wait_ge(ln1_load, LN1_ALL)
            V.tensor_scalar(ln1_gs[:, :], cols["ln1_g"][:, :], SCALE0, None, ALU.mult).then_inc(dve_shift, 1)
            norm1(0, first=True)
            low_weight("wk", wk_p, cols["ln1_g"])
            nxT_low(0)
            shifts_kq()
            low_weight("wq", wq_p, ln1_gs)
            low_weight("wv", wv_p, cols["ln1_g"])
            low_weight("wo", wo_p)
            shift_v()
            low_weight("w2", w2_p)
            k_low(0, 0)
            k_low(0, 1)
            shift_bo()
            q_low(0, 0)
            q_low(0, 1)
            shifts_up()
            for i, n in enumerate(("wq1", "wk1", "wv1")):
                l1_copy(i, n)
            low_weight("w1", w1_p, cols["ln2_g"])
            l1_low(0, "qk1", qk1_p, SCALE1)
            l1_low(1, "vo1", vo1_p, 1.0)
            dve.wait_ge(dve_lo, SPLIT["w1"])
            turn(1, 0, None, None)
            turn(2, 1, 0, None)
            turn(3, 2, 1, 0)
            with dve.Fori(3, GROUPS - 1) as g:
                turn(g + 1, g, g - 1, g - 2)
            turn(None, GROUPS - 1, GROUPS - 2, GROUPS - 3)
            turn(None, None, GROUPS - 1, GROUPS - 2)
            moments3(GROUPS - 1)
            norm3(GROUPS - 1)
            finish_last()

        @block.gpsimd
        def _(pool):
            P = nc.gpsimd
            P.memset(ident[:, :], 0.0).then_inc(consts, 1)
            pool.wait_ge(consts, 3)
            P.affine_select(out=ident[:, :], in_=ident[:, :], compare_op=ALU.not_equal, fill=1.0, base=0,
                            pattern=[[-1, 128]], channel_multiplier=1).then_inc(consts, 1)
            def rstd(n, g):
                pool.wait_ge(ln_dve[n], LN_STEPS * g + 9)
                P.tensor_tensor(lns[n]["rstd"][:, :], lns[n]["ve"][:, :], minus_half[:, :], ALU.pow).then_inc(ln_pool[n], 1)

            def bias(g):
                pool.wait_ge(adj_load, 16 * g + 16)
                pool.wait_ge(pool_pen1, g)
                pool.sem_inc(stand_pool, 1)
                P.tensor_copy(adj_f[:, :, :], adj_i[:, :, :]).then_inc(pool_adj, 1)
                pool.wait_ge(pool_adj, g + 1)
                pool.sem_inc(stand_pool, 1)
                P.tensor_scalar(pen0, adj_f[:, :, :], 0.0, MASKED, ALU.is_le, ALU.mult).then_inc(pool_bias, 1)
                pool.wait_ge(dve_s, 8 * g)
                pool.sem_inc(stand_pool, 1)
                P.tensor_scalar(bias0[:, :, :], adj_f[:, :, :], 0.1, None, ALU.mult).then_inc(pool_bias, 1)
                pool.wait_ge(pool_bias, 4 * g + 2)
                P.tensor_tensor(bias0[:, :, :], bias0[:, :, :], adj_f[:, :, :], ALU.mult).then_inc(pool_bias, 1)
                pool.wait_ge(pool_bias, 4 * g + 3)
                P.tensor_tensor(bias0[:, :, :], bias0[:, :, :], pen0, ALU.add).then_inc(pool_bias, 1)

            def x_plus_bo(g):
                pool.wait_ge(x_load, 16 * g + 16)
                pool.wait_ge(dve_x1, 4 * g)
                P.tensor_tensor(x_bo[:, :, :], xs[:, :, :],
                                rows["bo"][:, None, :].to_broadcast([128, PER, D]), ALU.add).then_inc(pool_xbo, 1)

            def mask1(g):
                pool.wait_ge(dve_s1, g)
                pool.sem_inc(stand_pool, 1)
                P.tensor_scalar(pen1[:, :, :], adj_f[:, :, :], 0.0, MASKED, ALU.is_equal, ALU.mult).then_inc(pool_pen1, 1)

            def x1_plus_b2(g):
                pool.wait_ge(ln_dve[2], LN_STEPS * g + LN_STEPS)
                P.tensor_tensor(x1[:, :, :], x1[:, :, :],
                                rows["b2"][:, None, :].to_broadcast([128, PER, D]), ALU.add).then_inc(pool_x1b, 1)

            def x2_plus_bo(g, steps):
                pool.wait_ge(pe_x2T, 2 * g + steps)
                P.tensor_tensor(x2[:, :, :], x2[:, :, :],
                                rows["bo1"][:, None, :].to_broadcast([128, PER, D]), ALU.add).then_inc(pool_x2b, 1)

            def finish(g, graphs=PER):
                pool.wait_ge(ln_dve[3], LN_STEPS * g + LN_STEPS - PER + graphs)
                P.tensor_tensor(y[:, 0:graphs, :], y[:, 0:graphs, :],
                                rows["gamma"][:, None, :].to_broadcast([128, graphs, D]), ALU.mult).then_inc(pool_out, 1)
                pool.wait_ge(pool_out, 2 * g + 1)
                P.tensor_tensor(y[:, 0:graphs, :], y[:, 0:graphs, :],
                                rows["beta"][:, None, :].to_broadcast([128, graphs, D]), ALU.add).then_inc(pool_out, 1)

            def turn(gp, ga, gb, gc):
                P, A, B, C = gp is not None, ga is not None, gb is not None, gc is not None
                if P:
                    rstd(1, gp)
                if C:
                    rstd(3, gc)
                    finish(gc)
                if B:
                    x2_plus_bo(gb, KT if A else PER)
                if A:
                    rstd(2, ga)
                    x1_plus_b2(ga)
                if P:
                    x_plus_bo(gp)
                if A:
                    mask1(ga)
                if P:
                    bias(gp)

            rstd(1, 0)
            bias(0)
            pool.wait_ge(dve_shift, 7)
            x_plus_bo(0)
            turn(1, 0, None, None)
            turn(2, 1, 0, None)
            turn(3, 2, 1, 0)
            with pool.Fori(3, GROUPS - 1) as g:
                turn(g + 1, g, g - 1, g - 2)
            turn(None, GROUPS - 1, GROUPS - 2, GROUPS - 3)
            turn(None, None, GROUPS - 1, GROUPS - 2)
            rstd(3, GROUPS - 1)
            finish(GROUPS - 1, PER // 2)


_INS = ['x', 'adj', 'L0_gnn_ln1_g', 'L0_gnn_ln1_b', 'L0_gnn_ln2_g', 'L0_gnn_ln2_b', 'L0_gnn_wq', 'L0_gnn_bq',
        'L0_gnn_wk', 'L0_gnn_bk', 'L0_gnn_wv', 'L0_gnn_bv', 'L0_gnn_wo', 'L0_gnn_bo', 'L0_gnn_w1', 'L0_gnn_b1',
        'L0_gnn_w2', 'L0_gnn_b2', 'L1_gnn_Wq', 'L1_gnn_Wk', 'L1_gnn_Wv', 'L1_gnn_Wo', 'L1_gnn_bo',
        'L1_gnn_gamma', 'L1_gnn_beta']


def kernel(**inputs):
    import numpy as _np
    import concourse.bacc as _bacc
    from concourse import mybir as _mybir
    from concourse.bass_utils import run_bass_kernel_spmd as _run

    nc = _bacc.Bacc("TRN2", target_bir_lowering=False, num_devices=1)
    arrays, args = {}, []
    for name in _INS:
        a = _np.ascontiguousarray(inputs[name])
        arrays[f"in_{name}"] = a
        args.append(nc.dram_tensor(f"in_{name}", a.shape, _mybir.dt.from_np(a.dtype), kind="ExternalInput").ap())
    args.append(nc.dram_tensor("out_0", (GRAPHS, NODES, D), _mybir.dt.float32, kind="ExternalOutput").ap())
    build(nc, *args)
    r = _run(nc, [arrays], core_ids=[0])
    return r.results[0]["out_0"]
```
